# Optimizing a Trainium2 kernel written in Bass

```python
import numpy as np
import jax
import jax.numpy as jnp

def _softmax(x, axis=-1):
    return jax.nn.softmax(x, axis=axis)

def _gelu(x):
    return jax.nn.gelu(x, approximate=True)

def _silu(x):
    return jax.nn.silu(x)

def _sigmoid(x):
    return jax.nn.sigmoid(x)

def _layernorm(x, axis=-1, eps=1e-05):
    m = jnp.mean(x, axis=axis, keepdims=True)
    v = jnp.var(x, axis=axis, keepdims=True)
    return (x - m) / jnp.sqrt(v + eps)

def _scatter_add(tgt, idx, src, axis=0):
    return tgt.at[idx].add(src)

def _segment_sum(src, seg, n):
    return jax.ops.segment_sum(src, seg, n)
kernel_name = 'mk_macaron_d2_jaxref_r8_3a17f7'

def setup_inputs(seed: int=0):
    np.random.seed(seed)
    _w = jnp.asarray

    def _L0_attn_setup():
        import jax, jax.numpy as jnp
        import numpy as np
        B, T, D = (1, 256, 128)
        H = 16
        SEM_DIM, GEO_DIM, ATTN_DIM = (64, 64, 128)
        ROPE_BASE = 10000.0
        NEG = -1000000000.0

        def _heads(y, hd):
            b, t, _ = y.shape
            return y.reshape(b, t, H, hd).transpose(0, 2, 1, 3)

        def _rope(x, cos, sin):
            hd = x.shape[-1]
            x1, x2 = (x[..., :hd // 2], x[..., hd // 2:])
            c = cos[None, None]
            sn = sin[None, None]
            return jnp.concatenate([x1 * c - x2 * sn, x2 * c + x1 * sn], axis=-1)

        def _forward(x, wq_sem, wk_sem, wq_geo, wk_geo, wv, wo, k_sem_null, k_geo_null, v_null):
            b, t, _ = x.shape
            sem_hd = wq_sem.shape[1] // H
            geo_hd = wq_geo.shape[1] // H
            v_hd = wv.shape[1] // H
            sem_scale = 1.0 / np.sqrt(sem_hd)
            geo_scale = 1.0 / np.sqrt(geo_hd)
            qs = _heads(x @ wq_sem, sem_hd)
            ks = _heads(x @ wk_sem, sem_hd)
            qg = _heads(x @ wq_geo, geo_hd)
            kg = _heads(x @ wk_geo, geo_hd)
            v = _heads(x @ wv, v_hd)
            pos = jnp.arange(t, dtype=jnp.float32)
            inv_freq = 1.0 / ROPE_BASE ** (jnp.arange(0, geo_hd, 2, dtype=jnp.float32) / geo_hd)
            ang = pos[:, None] * inv_freq[None, :]
            cos, sin = (jnp.cos(ang), jnp.sin(ang))
            qg = _rope(qg, cos, sin)
            kg = _rope(kg, cos, sin)
            ksn = jnp.broadcast_to(k_sem_null.reshape(1, 1, H, sem_hd).transpose(0, 2, 1, 3), (b, H, 1, sem_hd))
            kgn = jnp.broadcast_to(k_geo_null.reshape(1, 1, H, geo_hd).transpose(0, 2, 1, 3), (b, H, 1, geo_hd))
            vn = jnp.broadcast_to(v_null.reshape(1, 1, H, v_hd).transpose(0, 2, 1, 3), (b, H, 1, v_hd))
            ks_full = jnp.concatenate([ksn, ks], axis=2)
            kg_full = jnp.concatenate([kgn, kg], axis=2)
            v_full = jnp.concatenate([vn, v], axis=2)
            scores = jnp.einsum('bhqd,bhkd->bhqk', qs, ks_full).astype(jnp.float32) * sem_scale + jnp.einsum('bhqd,bhkd->bhqk', qg, kg_full).astype(jnp.float32) * geo_scale
            causal = jnp.tril(jnp.ones((t, t), dtype=bool))
            mask = jnp.concatenate([jnp.ones((t, 1), dtype=bool), causal], axis=1)
            scores = jnp.where(mask[None, None], scores, NEG)
            probs = jax.nn.softmax(scores, axis=-1).astype(v.dtype)
            out = jnp.einsum('bhqk,bhkd->bhqd', probs, v_full)
            out = out.transpose(0, 2, 1, 3).reshape(b, t, H * v_hd)
            return out @ wo
        key = jax.random.key(seed)
        ks = jax.random.split(key, 10)
        s = 0.02
        return {'x': jax.random.normal(ks[0], (B, T, D), jnp.float32), 'wq_sem': jax.random.normal(ks[1], (D, SEM_DIM), jnp.float32) * s, 'wk_sem': jax.random.normal(ks[2], (D, SEM_DIM), jnp.float32) * s, 'wq_geo': jax.random.normal(ks[3], (D, GEO_DIM), jnp.float32) * s, 'wk_geo': jax.random.normal(ks[4], (D, GEO_DIM), jnp.float32) * s, 'wv': jax.random.normal(ks[5], (D, ATTN_DIM), jnp.float32) * s, 'wo': jax.random.normal(ks[6], (ATTN_DIM, D), jnp.float32) * s, 'k_sem_null': jax.random.normal(ks[7], (SEM_DIM,), jnp.float32) * s, 'k_geo_null': jax.random.normal(ks[8], (GEO_DIM,), jnp.float32) * s, 'v_null': jax.random.normal(ks[9], (ATTN_DIM,), jnp.float32) * s}
    _L0_attn_in = _L0_attn_setup()

    def _L0_ffn_setup():
        import jax, jax.numpy as jnp
        import numpy as np
        DIM = 128
        NUM_EXPERTS = 8
        TOP_K = 2
        HIDDEN = 4 * DIM // TOP_K
        BS, SLEN = (1, 256)

        def _moe(x, gate_w, w_up, w_down, expert_bias):
            bs, slen, dim = x.shape
            xf = x.reshape(-1, dim)
            scores = jax.nn.sigmoid(xf @ gate_w.T)
            biased = scores + expert_bias
            _, sel = jax.lax.top_k(biased, TOP_K)
            top_scores = jnp.take_along_axis(scores, sel, axis=-1)

            def body(acc, ew):
                e, wu, wd = ew
                w_t = jnp.sum(jnp.where(sel == e, top_scores, 0.0), axis=-1)
                xe = xf * w_t[:, None]
                h = jnp.square(jax.nn.relu(xe @ wu.T))
                return (acc + h @ wd.T, None)
            out0 = jnp.zeros_like(xf)
            out, _ = jax.lax.scan(body, out0, (jnp.arange(NUM_EXPERTS), w_up, w_down))
            return out.reshape(bs, slen, dim)
        key = jax.random.key(seed)
        k0, k1, k2, k3 = jax.random.split(key, 4)
        x = jax.random.normal(k0, (BS, SLEN, DIM), dtype=jnp.float32)
        gate_w = jax.random.normal(k1, (NUM_EXPERTS, DIM), dtype=jnp.float32) * 0.02
        w_up = jax.random.normal(k2, (NUM_EXPERTS, HIDDEN, DIM), dtype=jnp.float32) * 0.02
        w_down = jax.random.normal(k3, (NUM_EXPERTS, DIM, HIDDEN), dtype=jnp.float32) * 0.02
        expert_bias = jnp.zeros((NUM_EXPERTS,), dtype=jnp.float32)
        return {'x': x, 'gate_w': gate_w, 'w_up': w_up, 'w_down': w_down, 'expert_bias': expert_bias}
    _L0_ffn_in = _L0_ffn_setup()

    def _L1_attn_setup():
        import jax, jax.numpy as jnp
        import numpy as np
        N_HEADS = 16
        MAX_LEN = 128
        key = jax.random.key(seed)
        ks = jax.random.split(key, 6)
        B, T, C = (4, 128, 128)
        scale = 0.02
        return {'x': jax.random.normal(ks[0], (B, T, C), dtype=jnp.float32), 'qkv_w': jax.random.normal(ks[1], (3 * C, C), dtype=jnp.float32) * scale, 'qkv_b': jax.random.normal(ks[2], (3 * C,), dtype=jnp.float32) * scale, 'proj_w': jax.random.normal(ks[3], (C, C), dtype=jnp.float32) * scale, 'proj_b': jax.random.normal(ks[4], (C,), dtype=jnp.float32) * scale, 'rel_pos_emb': jax.random.normal(ks[5], (2 * MAX_LEN - 1, C), dtype=jnp.float32) * scale}
    _L1_attn_in = _L1_attn_setup()

    def _L1_ffn_setup():
        import jax, jax.numpy as jnp
        import numpy as np
        B, S, D, E, K = (2, 256, 128, 8, 2)
        H = 4 * D
        key = jax.random.key(seed)
        ks = jax.random.split(key, 6)
        x = jax.random.normal(ks[0], (B, S, D), dtype=jnp.float32)
        lim_g = np.sqrt(6.0 / (D + E)).astype(np.float32)
        W_gate = jax.random.uniform(ks[1], (D, E), minval=-lim_g, maxval=lim_g, dtype=jnp.float32)
        lim1 = np.sqrt(1.0 / D).astype(np.float32)
        lim2 = np.sqrt(1.0 / H).astype(np.float32)
        W1 = jax.random.uniform(ks[2], (E, D, H), minval=-lim1, maxval=lim1, dtype=jnp.float32)
        b1 = jax.random.uniform(ks[3], (E, H), minval=-lim1, maxval=lim1, dtype=jnp.float32)
        W2 = jax.random.uniform(ks[4], (E, H, D), minval=-lim2, maxval=lim2, dtype=jnp.float32)
        b2 = jax.random.uniform(ks[5], (E, D), minval=-lim2, maxval=lim2, dtype=jnp.float32)
        return {'x': x, 'W_gate': W_gate, 'W1': W1, 'b1': b1, 'W2': W2, 'b2': b2}
    _L1_ffn_in = _L1_ffn_setup()
    _d = {'L0_attn_x': _L0_attn_in['x'], 'L0_attn_wq_sem': _L0_attn_in['wq_sem'], 'L0_attn_wk_sem': _L0_attn_in['wk_sem'], 'L0_attn_wq_geo': _L0_attn_in['wq_geo'], 'L0_attn_wk_geo': _L0_attn_in['wk_geo'], 'L0_attn_wv': _L0_attn_in['wv'], 'L0_attn_wo': _L0_attn_in['wo'], 'L0_attn_k_sem_null': _L0_attn_in['k_sem_null'], 'L0_attn_k_geo_null': _L0_attn_in['k_geo_null'], 'L0_attn_v_null': _L0_attn_in['v_null'], 'L0_ffn_gate_w': _L0_ffn_in['gate_w'], 'L0_ffn_w_up': _L0_ffn_in['w_up'], 'L0_ffn_w_down': _L0_ffn_in['w_down'], 'L0_ffn_expert_bias': _L0_ffn_in['expert_bias'], 'L1_attn_qkv_w': _L1_attn_in['qkv_w'], 'L1_attn_qkv_b': _L1_attn_in['qkv_b'], 'L1_attn_proj_w': _L1_attn_in['proj_w'], 'L1_attn_proj_b': _L1_attn_in['proj_b'], 'L1_attn_rel_pos_emb': _L1_attn_in['rel_pos_emb'], 'L1_ffn_W_gate': _L1_ffn_in['W_gate'], 'L1_ffn_W1': _L1_ffn_in['W1'], 'L1_ffn_b1': _L1_ffn_in['b1'], 'L1_ffn_W2': _L1_ffn_in['W2'], 'L1_ffn_b2': _L1_ffn_in['b2']}
    _x0 = _d['L0_attn_x']
    _d['L0_attn_x'] = jax.random.normal(jax.random.fold_in(jax.random.key(seed), 1), (16, 256, 128), dtype=_x0.dtype)
    del _x0
    return _d

def reference(L0_attn_x, L0_attn_wq_sem, L0_attn_wk_sem, L0_attn_wq_geo, L0_attn_wk_geo, L0_attn_wv, L0_attn_wo, L0_attn_k_sem_null, L0_attn_k_geo_null, L0_attn_v_null, L0_ffn_gate_w, L0_ffn_w_up, L0_ffn_w_down, L0_ffn_expert_bias, L1_attn_qkv_w, L1_attn_qkv_b, L1_attn_proj_w, L1_attn_proj_b, L1_attn_rel_pos_emb, L1_ffn_W_gate, L1_ffn_W1, L1_ffn_b1, L1_ffn_W2, L1_ffn_b2):

    def _L0_attn_ref(x, wq_sem, wk_sem, wq_geo, wk_geo, wv, wo, k_sem_null, k_geo_null, v_null):
        import jax, jax.numpy as jnp
        import numpy as np
        B, T, D = (1, 256, 128)
        H = 16
        SEM_DIM, GEO_DIM, ATTN_DIM = (64, 64, 128)
        ROPE_BASE = 10000.0
        NEG = -1000000000.0

        def _heads(y, hd):
            b, t, _ = y.shape
            return y.reshape(b, t, H, hd).transpose(0, 2, 1, 3)

        def _rope(x, cos, sin):
            hd = x.shape[-1]
            x1, x2 = (x[..., :hd // 2], x[..., hd // 2:])
            c = cos[None, None]
            sn = sin[None, None]
            return jnp.concatenate([x1 * c - x2 * sn, x2 * c + x1 * sn], axis=-1)

        def _forward(x, wq_sem, wk_sem, wq_geo, wk_geo, wv, wo, k_sem_null, k_geo_null, v_null):
            b, t, _ = x.shape
            sem_hd = wq_sem.shape[1] // H
            geo_hd = wq_geo.shape[1] // H
            v_hd = wv.shape[1] // H
            sem_scale = 1.0 / np.sqrt(sem_hd)
            geo_scale = 1.0 / np.sqrt(geo_hd)
            qs = _heads(x @ wq_sem, sem_hd)
            ks = _heads(x @ wk_sem, sem_hd)
            qg = _heads(x @ wq_geo, geo_hd)
            kg = _heads(x @ wk_geo, geo_hd)
            v = _heads(x @ wv, v_hd)
            pos = jnp.arange(t, dtype=jnp.float32)
            inv_freq = 1.0 / ROPE_BASE ** (jnp.arange(0, geo_hd, 2, dtype=jnp.float32) / geo_hd)
            ang = pos[:, None] * inv_freq[None, :]
            cos, sin = (jnp.cos(ang), jnp.sin(ang))
            qg = _rope(qg, cos, sin)
            kg = _rope(kg, cos, sin)
            ksn = jnp.broadcast_to(k_sem_null.reshape(1, 1, H, sem_hd).transpose(0, 2, 1, 3), (b, H, 1, sem_hd))
            kgn = jnp.broadcast_to(k_geo_null.reshape(1, 1, H, geo_hd).transpose(0, 2, 1, 3), (b, H, 1, geo_hd))
            vn = jnp.broadcast_to(v_null.reshape(1, 1, H, v_hd).transpose(0, 2, 1, 3), (b, H, 1, v_hd))
            ks_full = jnp.concatenate([ksn, ks], axis=2)
            kg_full = jnp.concatenate([kgn, kg], axis=2)
            v_full = jnp.concatenate([vn, v], axis=2)
            scores = jnp.einsum('bhqd,bhkd->bhqk', qs, ks_full).astype(jnp.float32) * sem_scale + jnp.einsum('bhqd,bhkd->bhqk', qg, kg_full).astype(jnp.float32) * geo_scale
            causal = jnp.tril(jnp.ones((t, t), dtype=bool))
            mask = jnp.concatenate([jnp.ones((t, 1), dtype=bool), causal], axis=1)
            scores = jnp.where(mask[None, None], scores, NEG)
            probs = jax.nn.softmax(scores, axis=-1).astype(v.dtype)
            out = jnp.einsum('bhqk,bhkd->bhqd', probs, v_full)
            out = out.transpose(0, 2, 1, 3).reshape(b, t, H * v_hd)
            return out @ wo
        return _forward(x, wq_sem, wk_sem, wq_geo, wk_geo, wv, wo, k_sem_null, k_geo_null, v_null)

    def _L0_ffn_ref(x, gate_w, w_up, w_down, expert_bias):
        import jax, jax.numpy as jnp
        import numpy as np
        DIM = 128
        NUM_EXPERTS = 8
        TOP_K = 2
        HIDDEN = 4 * DIM // TOP_K
        BS, SLEN = (1, 256)

        def _moe(x, gate_w, w_up, w_down, expert_bias):
            bs, slen, dim = x.shape
            xf = x.reshape(-1, dim)
            scores = jax.nn.sigmoid(xf @ gate_w.T)
            biased = scores + expert_bias
            _, sel = jax.lax.top_k(biased, TOP_K)
            top_scores = jnp.take_along_axis(scores, sel, axis=-1)

            def body(acc, ew):
                e, wu, wd = ew
                w_t = jnp.sum(jnp.where(sel == e, top_scores, 0.0), axis=-1)
                xe = xf * w_t[:, None]
                h = jnp.square(jax.nn.relu(xe @ wu.T))
                return (acc + h @ wd.T, None)
            out0 = jnp.zeros_like(xf)
            out, _ = jax.lax.scan(body, out0, (jnp.arange(NUM_EXPERTS), w_up, w_down))
            return out.reshape(bs, slen, dim)
        return _moe(x, gate_w, w_up, w_down, expert_bias)

    def _L1_attn_ref(x, qkv_w, qkv_b, proj_w, proj_b, rel_pos_emb):
        import jax, jax.numpy as jnp
        import numpy as np
        N_HEADS = 16
        MAX_LEN = 128
        B, T, C = x.shape
        H = N_HEADS
        D = C // H
        qkv = (x @ qkv_w.T + qkv_b).reshape(B, T, 3, H, D)
        qkv = jnp.transpose(qkv, (2, 0, 3, 1, 4))
        q, k, v = (qkv[0], qkv[1], qkv[2])
        att = jnp.einsum('bhtd,bhsd->bhts', q, k) / np.sqrt(D).astype(np.float32)
        table = rel_pos_emb.reshape(2 * MAX_LEN - 1, H, D).sum(axis=-1)
        pos = jnp.arange(T)
        rel_idx = pos[:, None] - pos[None, :] + (MAX_LEN - 1)
        bias = jnp.transpose(table[rel_idx], (2, 0, 1))
        att = att + bias[None]
        causal = pos[None, :] > pos[:, None]
        att = jnp.where(causal[None, None], -jnp.inf, att)
        att = jax.nn.softmax(att, axis=-1)
        out = jnp.einsum('bhts,bhsd->bhtd', att, v)
        out = jnp.transpose(out, (0, 2, 1, 3)).reshape(B, T, C)
        return out @ proj_w.T + proj_b

    def _L1_ffn_ref(x, W_gate, W1, b1, W2, b2):
        import jax, jax.numpy as jnp
        import numpy as np
        B, S, D, E, K = (2, 256, 128, 8, 2)
        H = 4 * D
        gate = jnp.einsum('bsd,de->bse', x, W_gate)
        kth = jax.lax.top_k(gate, K)[0][..., -1:]
        mask = jax.nn.softmax(jnp.where(gate >= kth, gate, -jnp.inf), axis=-1)
        h = jax.nn.relu(jnp.einsum('bsd,edh->bseh', x, W1) + b1)
        y = jnp.einsum('bseh,ehd->bsed', h, W2) + b2
        return (y * mask[..., None]).mean(axis=-2)
    x = L0_attn_x
    x = x + 0.5 * _L0_ffn_ref(_layernorm(x, axis=-1), L0_ffn_gate_w, L0_ffn_w_up, L0_ffn_w_down, L0_ffn_expert_bias)
    x = x + _L0_attn_ref(_layernorm(x, axis=-1), L0_attn_wq_sem, L0_attn_wk_sem, L0_attn_wq_geo, L0_attn_wk_geo, L0_attn_wv, L0_attn_wo, L0_attn_k_sem_null, L0_attn_k_geo_null, L0_attn_v_null)
    x = x + 0.5 * _L0_ffn_ref(_layernorm(x, axis=-1), L0_ffn_gate_w, L0_ffn_w_up, L0_ffn_w_down, L0_ffn_expert_bias)
    x = x + 0.5 * _L1_ffn_ref(_layernorm(x, axis=-1), L1_ffn_W_gate, L1_ffn_W1, L1_ffn_b1, L1_ffn_W2, L1_ffn_b2)
    x = x + _L1_attn_ref(_layernorm(x, axis=-1), L1_attn_qkv_w, L1_attn_qkv_b, L1_attn_proj_w, L1_attn_proj_b, L1_attn_rel_pos_emb)
    x = x + 0.5 * _L1_ffn_ref(_layernorm(x, axis=-1), L1_ffn_W_gate, L1_ffn_W1, L1_ffn_b1, L1_ffn_W2, L1_ffn_b2)
    return x

_drawn_inputs = setup_inputs


def setup_inputs(seed=0):
    import zlib

    import numpy as np

    out = dict(_drawn_inputs(seed))
    spreads = {'L0_ffn_expert_bias': (0.0, 0.8)}
    factors = {'L0_attn_wq_sem': 8.0,
     'L0_attn_wk_sem': 8.0,
     'L0_attn_wq_geo': 8.0,
     'L0_attn_wk_geo': 8.0,
     'L0_attn_wv': 8.0,
     'L0_attn_wo': 8.0,
     'L0_attn_k_sem_null': 64.0,
     'L0_attn_k_geo_null': 64.0,
     'L0_attn_v_null': 53.409,
     'L0_ffn_gate_w': 8.0,
     'L0_ffn_w_up': 7.715,
     'L0_ffn_w_down': 7.076,
     'L1_attn_qkv_w': 7.064,
     'L1_attn_qkv_b': 8.0,
     'L1_attn_proj_w': 5.921,
     'L1_attn_proj_b': 14.73,
     'L1_attn_rel_pos_emb': 8.0,
     'L1_ffn_W_gate': 11.636,
     'L1_ffn_W1': 14.148,
     'L1_ffn_b1': 64.0,
     'L1_ffn_b2': 64.0,
     'L1_ffn_W2': 3.78}
    for name, (base, spread) in spreads.items():
        noise = np.random.default_rng([zlib.crc32(name.encode()), seed]).standard_normal(out[name].shape)
        drawn = base * np.exp(spread * noise) if base else spread * noise
        out[name] = jnp.asarray(drawn.astype(out[name].dtype))
    for name, factor in factors.items():
        out[name] = (out[name] * factor).astype(out[name].dtype)
    return out
```

```python
from collections import namedtuple
from contextlib import ExitStack

import numpy as np

import concourse.bass as bass
from concourse import mybir

fp32 = mybir.dt.float32
fp32r = mybir.dt.float32r
bf16 = mybir.dt.bfloat16
ALU = mybir.AluOpType
ACT = mybir.ActivationFunctionType
AX = mybir.AxisListType

P = 128
D = 128
T = 256
B = 16
CT = 4
CW = CT * P
NCH = B * T // CW
E = 8
TOP_K = 2
LN_EPS = 1e-5
NPARTS = 3
WR = NPARTS * NPARTS * E

LAG = 3
AT_STATS, AT_NORM, AT_Y, AT_XT, AT_SPLIT, AT_GATE, AT_ROUTE, AT_EXP, AT_ROUTE2, AT_W = 1, 3, 5, 7, 8, 9, 10, 11, 12, 14
LINKS = 20


def group(**named):
    return namedtuple("Group", named)(**named)


class Buffers:
    pass


def reached(eng, sem, value):
    if not isinstance(value, int) or value > 0:
        eng.wait_ge(sem, value)


class Link:

    def __init__(self, eng, sem, chunk):
        self.eng, self.sem, self.at, self.taken = eng, sem, chunk * LINKS, 0

    def __call__(self, instruction):
        self.at, self.taken = self.at + 1, self.taken + 1
        instruction.then_inc(self.sem, 1)
        self.eng.wait_ge(self.sem, self.at)

    def close(self):
        self.eng.sem_inc(self.sem, LINKS - self.taken)


def tiles(x, c, n):
    return x[:, bass.ds(c * n, n), :]


def over_pairs(eng, body, start, count):
    body(start, 0, True, False)
    body(start + 1, 1, False, False)
    with eng.Fori(start // 2 + 1, (start + count) // 2 - 1) as i:
        body(2 * i, 0, False, False)
        body(2 * i + 1, 1, False, False)
    body(start + count - 2, 0, False, False)
    body(start + count - 1, 1, False, True)


FFN_SEMS = ("stats_step link pool_link stats_ready rstd_ready xn_ready xT_psum xT_ready xsplit_ready gate_psum gate_in gate_exp "
            "w_ready wT_psum wT_ready wb_full up_full relu_full scaled_full h_full down_done y_full yT_ready y_psum x_done")


def ffn_pe(nc, pe, s, g, f, m, c0):
    NBK = E * f.nb
    mm = nc.tensor.matmul

    def transpose_x(c):
        pe.wait_ge(s.xn_ready, c + 1)
        for t in range(CT):
            i = nc.tensor.transpose(m.misc[:, t * P:(t + 1) * P], m.xn[:, t, :], g.ident[:, :])
        i.then_inc(s.xT_psum, 1)

    def gates(c):
        pe.wait_ge(s.xT_ready, c + 1)
        for t in range(CT):
            i = mm(m.misc[:, t * E:(t + 1) * E], m.xT[:, t * P:(t + 1) * P], f.gate[:, :], start=True, stop=True)
        i.then_inc(s.gate_psum, 1)

    def transpose_w(c):
        pe.wait_ge(s.w_ready, c + 1)
        for t in range(CT):
            i = nc.tensor.transpose(m.misc_bf[0:WR, t * P:(t + 1) * P], m.wparts_flat[:, t, :], g.ident_bf[:, :])
        i.then_inc(s.wT_psum, 1)

    def transpose_y(c):
        pe.wait_ge(s.yT_ready, c + 1)
        for t in range(CT):
            i = nc.tensor.transpose(m.misc[:, t * P:(t + 1) * P], m.yT[:, t * P:(t + 1) * P], g.ident[:, :])
        i.then_inc(s.y_psum, 1)

    def down(c, par, k):
        if k == 0:
            reached(pe, s.yT_ready, c)
        pe.wait_ge(s.h_full if f.square else s.scaled_full, c * NBK + k + 1)
        last = k == NBK - 1
        i = mm(m.y[:, :], f.down[:, k, :], m.h[:, k % m.NH, :], start=k == 0, stop=last and f.b2 is None)
        i.then_inc(s.down_done, 1)
        if last and f.b2 is not None:
            mm(m.y[:, :], f.b2[0:WR, :], m.wT[0:WR, par, :], start=False, stop=True).then_inc(s.y_full, 1)

    def main(c, par, first, last):
        for k in range(NBK):
            e, hb = divmod(k, f.nb)
            if hb == 0:
                if e == 0:
                    pe.wait_ge(s.wT_ready, c + 1)
                reached(pe, s.scaled_full, (c * E + e - 1) * f.nb)
                mm(m.wb[e % 2][:, :], g.pick[0:WR, e, :], m.wT[0:WR, par, :], start=True, stop=True).then_inc(s.wb_full, 1)
            if k == 0:
                pe.wait_ge(s.xsplit_ready, c + 1)
            if not (first and k < m.NU):
                pe.wait_ge(s.relu_full, c * NBK + k + 1 - m.NU)
            u = m.up[k % m.NU]
            mm(u[:, :], f.up_hi[:, k, :], m.x_hi[:, par, :], start=True, stop=False)
            mm(u[:, :], f.up_hi[:, k, :], m.x_lo[:, par, :], start=False, stop=False)
            mm(u[:, :], f.up_lo[:, k, :], m.x_hi[:, par, :], start=False, stop=True).then_inc(s.up_full, 1)
            if k >= LAG:
                down(c, par, k - LAG)
            elif not first:
                down(c - 1, 1 - par, k - LAG + NBK)
            if k == AT_Y and not first:
                transpose_y(c - 1)
            if not last:
                if k == AT_XT:
                    reached(pe, s.x_done, c)
                    transpose_x(c + 1)
                if k == AT_GATE:
                    gates(c + 1)
                if k == AT_W:
                    transpose_w(c + 1)

    transpose_x(c0)
    gates(c0)
    transpose_w(c0)
    over_pairs(pe, main, c0, NCH)
    for k in range(NBK - LAG, NBK):
        down(c0 + NCH - 1, 1, k)
    transpose_y(c0 + NCH - 1)


def ffn_act(nc, act, s, g, f, m, c0, also=None):
    NBK = E * f.nb

    def copy_xT(c):
        act.wait_ge(s.xT_psum, c + 1)
        reached(act, s.gate_psum, c)
        reached(act, s.xsplit_ready, c)
        nc.scalar.copy(m.xT[:, :], m.misc[:, :]).then_inc(s.xT_ready, 1)

    def gate_exp(c):
        reached(act, s.w_ready, c)
        if f.sigmoid:
            act.wait_ge(s.gate_psum, c + 1)
            nc.scalar.activation(m.gexp[:, :], m.misc[:, 0:CT * E], ACT.Exp, scale=-1.0).then_inc(s.gate_exp, 1)
        else:
            act.wait_ge(s.gate_in, c + 1)
            nc.scalar.activation(m.gexp[:, :], m.gsub[:, :], ACT.Exp).then_inc(s.gate_exp, 1)

    def copy_wT(c, par):
        act.wait_ge(s.wT_psum, c + 1)
        reached(act, s.wb_full, (c - 1) * E)
        reached(act, s.down_done, (c - 1) * NBK)
        if f.b2 is not None:
            reached(act, s.y_full, c - 1)
        nc.scalar.copy(m.wT[0:WR, par, :], m.misc_bf[0:WR, 0:CW]).then_inc(s.wT_ready, 1)

    def copy_y(c):
        if f.b2 is not None:
            act.wait_ge(s.y_full, c + 1)
        act.wait_ge(s.down_done, (c + 1) * NBK)
        reached(act, s.y_psum, c)
        nc.scalar.copy(m.yT[:, :], m.y[:, :]).then_inc(s.yT_ready, 1)

    def main(c, par, first, last):
        for k in range(NBK):
            act.wait_ge(s.up_full, c * NBK + k + 1)
            if not (first and k < m.NR):
                act.wait_ge(s.scaled_full, c * NBK + k + 1 - m.NR)
            if f.b1 is None:
                i = nc.scalar.activation(m.relu[:, k % m.NR, :], m.up[k % m.NU][:, :], ACT.Relu)
            else:
                i = nc.scalar.activation(m.relu[:, k % m.NR, :], m.up[k % m.NU][:, :], ACT.Relu, bias=f.b1[:, k:k + 1])
            i.then_inc(s.relu_full, 1)
            if k == LAG and not first:
                copy_y(c - 1)
            if k == AT_SPLIT and also is not None:
                if first:
                    act.wait_ge(also.loaded, 32)
                nc.scalar.copy(also.hi[:, bass.ds(c * CT, CT), :], also.raw[:, bass.ds(c * CT, CT), :]).then_inc(also.hi_done, 1)
            if not last:
                if k == AT_XT:
                    copy_xT(c + 1)
                if k == AT_EXP:
                    gate_exp(c + 1)
                if k == AT_W:
                    copy_wT(c + 1, 1 - par)

    copy_xT(c0)
    gate_exp(c0)
    copy_wT(c0, 0)
    over_pairs(act, main, c0, NCH)
    copy_y(c0 + NCH - 1)


def ffn_pool(nc, pool, s, g, f, m, c0):
    NBK = E * f.nb

    def rstd(c):
        pool.wait_ge(s.stats_ready, c + 1)
        reached(pool, s.xn_ready, c)
        nc.gpsimd.tensor_tensor(m.vare[:, :], m.mv[:, :, 1], g.eps[:, 0:CT], ALU.add).then_inc(s.pool_link, 1)
        pool.wait_ge(s.pool_link, c + 1)
        nc.gpsimd.tensor_tensor(m.rstd[:, :], m.vare[:, :], g.neg_half[:, 0:CT], ALU.pow).then_inc(s.rstd_ready, 1)

    def main(c, par, first, last):
        for k in range(NBK):
            if k == AT_STATS + 1 and not last:
                rstd(c + 1)
            if f.square:
                pool.wait_ge(s.scaled_full, c * NBK + k + 1)
                if not (first and k < m.NH):
                    pool.wait_ge(s.down_done, c * NBK + k + 1 - m.NH)
                q = m.scaled[:, k % m.NS, :]
                nc.gpsimd.tensor_tensor(m.h[:, k % m.NH, :], q, q, ALU.mult).then_inc(s.h_full, 1)

    rstd(c0)
    over_pairs(pool, main, c0, NCH)


def ffn_dve(nc, dve, s, g, f, m, c0, x_before, also=None):
    NBK = E * f.nb
    v = nc.vector

    def stats(c):
        reached(dve, s.rstd_ready, c)
        for t in range(CT):
            i = v.bn_stats(m.bn[:, t, :], g.x[:, bass.ds((c - c0) * CT + t, 1), :][:, 0, :])
        i.then_inc(s.stats_step, 1)

    def aggregate(c):
        for t in range(CT):
            i = v.bn_aggr(m.mv[:, t, :], m.bn[:, t, :])
        i.then_inc(s.stats_ready, 1)

    def norm(c):
        dve.wait_ge(s.rstd_ready, c + 1)
        dve.wait_ge(s.stats_ready, c + 1)
        reached(dve, s.xT_psum, c)
        for t in range(CT):
            i = v.tensor_scalar(m.xn[:, t, :], g.x[:, bass.ds((c - c0) * CT + t, 1), :][:, 0, :], m.mv[:, t, 0:1],
                                m.rstd[:, t:t + 1], ALU.subtract, ALU.mult)
        i.then_inc(s.xn_ready, 1)

    def split(c, par, link):
        dve.wait_ge(s.xT_ready, c + 1)
        reached(dve, s.up_full, (c - 1) * NBK)
        link(v.tensor_copy(m.x_hi[:, par, :], m.xT[:, :]))
        v.tensor_tensor(m.x_lo[:, par, :], m.xT[:, :], m.x_hi[:, par, :].bitcast(fp32), ALU.subtract).then_inc(s.xsplit_ready, 1)

    def route(c, link):
        if f.sigmoid:
            return
        dve.wait_ge(s.gate_psum, c + 1)
        v.tensor_copy(m.glog[:, :, :], m.misc[:, 0:CT * E].rearrange("p (t e) -> p t e", e=E))
        for t in range(CT):
            i = v.max(m.gmax[:, t, :], m.misc[:, t * E:(t + 1) * E])
        link(i)
        reached(dve, s.gate_exp, c)
        v.tensor_tensor(m.gsub[:, :].rearrange("p (t e) -> p t e", e=E), m.glog[:, :, :],
                        m.gmax[:, :, 0:1].broadcast_to([P, CT, E]), ALU.subtract).then_inc(s.gate_in, 1)
        link(v.tensor_tensor(m.chosen[:, :, :], m.glog[:, :, :],
                             m.gmax[:, :, TOP_K - 1:TOP_K].broadcast_to([P, CT, E]), ALU.is_ge))

    def route2(c, link):
        dve.wait_ge(s.gate_exp, c + 1)
        if f.sigmoid:
            link(v.tensor_scalar(m.gsub[:, :], m.gexp[:, :], 1.0, None, ALU.add))
            link(v.reciprocal(m.glog_flat[:, :], m.gsub[:, :]))
            link(v.tensor_tensor(m.biased[:, :, :], m.glog[:, :, :],
                                 f.expert_bias[:, :].unsqueeze(1).broadcast_to([P, CT, E]), ALU.add))
            for t in range(CT):
                other = m.biased[:, t, :].unsqueeze(1).broadcast_to([P, E, E])
                own = m.biased[:, t, :].unsqueeze(2).broadcast_to([P, E, E])
                v.tensor_tensor(m.ahead[:, t, :, :], other, own, ALU.is_gt)
                i = v.tensor_tensor(m.tied[:, t, :, :], other, own, ALU.is_equal)
            link(i)
            link(v.tensor_tensor(m.tied[:, :, :, :].rearrange("p t a b -> p t (a b)"),
                                 m.tied[:, :, :, :].rearrange("p t a b -> p t (a b)"),
                                 g.lower[:, :].unsqueeze(1).broadcast_to([P, CT, E * E]), ALU.mult))
            link(v.tensor_tensor(m.ahead[:, :, :, :], m.ahead[:, :, :, :], m.tied[:, :, :, :], ALU.add))
            link(v.tensor_reduce(m.rank[:, :, :], m.ahead[:, :, :, :], AX.X, ALU.add))
            link(v.scalar_tensor_tensor(out=m.w[:, :, :], in0=m.rank[:, :, :], scalar=float(TOP_K), in1=m.glog[:, :, :],
                                        op0=ALU.is_lt, op1=ALU.mult))
        else:
            link(v.tensor_tensor(m.w[:, :, :], m.gexp[:, :].rearrange("p (t e) -> p t e", e=E), m.chosen[:, :, :], ALU.mult))
            link(v.tensor_reduce(m.wsum[:, :], m.w[:, :, :], AX.X, ALU.add))
            link(v.reciprocal(m.wrec[:, :], m.wsum[:, :]))
            link(v.tensor_tensor(m.w[:, :, :], m.w[:, :, :], m.wrec[:, :].unsqueeze(2).broadcast_to([P, CT, E]), ALU.mult))
        reached(dve, s.wT_psum, c)
        for a in range(NPARTS):
            for b in range(NPARTS):
                i = v.tensor_copy(m.wparts[:, :, b, a, :], m.w[:, :, :])
            if a < NPARTS - 1:
                link(i)
                link(v.tensor_tensor(m.w[:, :, :], m.w[:, :, :], m.wparts[:, :, 0, a, :], ALU.subtract))
        i.then_inc(s.w_ready, 1)

    def update(c):
        dve.wait_ge(s.y_psum, c + 1)
        rows = tiles(g.x, c - c0, CT)
        v.scalar_tensor_tensor(out=rows, in0=m.misc[:, :].rearrange("p (t d) -> p t d", d=D), scalar=f.scale, in1=rows,
                               op0=ALU.mult, op1=ALU.add).then_inc(s.x_done, 1)

    def links_of(c):
        return Link(dve, s.link, c)

    def prepare(c, par, link):
        stats(c)
        dve.wait_ge(s.stats_step, c + 1)
        aggregate(c)
        norm(c)
        split(c, par, link)
        route(c, link)
        route2(c, link)
        link.close()

    def main(c, par, first, last):
        link = Link(dve, s.link, c + 1)
        for k in range(NBK):
            e, hb = divmod(k, f.nb)
            if hb == 0:
                dve.wait_ge(s.wb_full, c * E + e + 1)
            dve.wait_ge(s.relu_full, c * NBK + k + 1)
            if k == AT_STATS + 1 and not last:
                dve.wait_ge(s.stats_step, c + 2)
            if f.square:
                if not (first and k < m.NS):
                    dve.wait_ge(s.h_full, c * NBK + k + 1 - m.NS)
                out, full = m.scaled[:, k % m.NS, :], s.scaled_full
            else:
                if not (first and k < m.NH):
                    dve.wait_ge(s.down_done, c * NBK + k + 1 - m.NH)
                out, full = m.h[:, k % m.NH, :], s.scaled_full
            v.tensor_tensor(out, m.relu[:, k % m.NR, :], m.wb[e % 2][:, :], ALU.mult).then_inc(full, 1)
            if k == AT_STATS + 1 and not last:
                aggregate(c + 1)
            if k == AT_Y and not first:
                update(c - 1)
            if k == AT_W and also is not None:
                dve.wait_ge(also.hi_done, c + 1)
                part = bass.ds(c * CT, CT)
                v.tensor_tensor(also.lo[:, part, :], also.raw[:, part, :], also.hi[:, part, :].bitcast(fp32),
                                ALU.subtract).then_inc(also.lo_done, 1)
            if not last:
                if k == AT_STATS:
                    stats(c + 1)
                if k == AT_NORM:
                    norm(c + 1)
                if k == AT_SPLIT:
                    split(c + 1, 1 - par, link)
                if k == AT_ROUTE:
                    route(c + 1, link)
                if k == AT_ROUTE2:
                    route2(c + 1, link)
                    link.close()

    x_before(dve)
    prepare(c0, 0, Link(dve, s.link, c0))
    over_pairs(dve, main, c0, NCH)
    update(c0 + NCH - 1)


H = 16
HD = D // H
ST = T // P
SLOT = 32
HPS = P // SLOT
SETS = H // HPS
PAIRS = H // 2
HC = T + P
P2, PV = 4, 5
KQ = 3 * HD
NEG = -1.0e30
LEAST = -3.0e38
ATTN_SEMS = ("stats_step stats_ready pool_link rstd_ready xn_ready xT_psum xT_ready proj_psum proj_step proj_read hi_staged lo_staged slots_clear "
             "stage_ready null_prod null_score values_ready kq_psum kq_act kq_dve s1_full s1_read slot_step slots_ready max_psum "
             "q2_ready s2_full s2_biased p_raw p_ready pv_done o_copied ob_psum null_in null_exp nulls_ready fin_step "
             "rows_biased att_ready aT_psum aT_ready y_psum x_done o_clear")


def over_sequences(eng, body):
    def has(b, loop=False):
        return group(cur=loop or b < B, nxt=loop or b + 1 < B, prev=loop or 1 <= b <= B, prev2=loop or b >= 2, ever=loop or b > 0)

    body(0, 0, has(0))
    body(1, 1, has(1))
    with eng.Fori(1, B // 2 - 1) as i:
        body(2 * i, 0, has(0, True))
        body(2 * i + 1, 1, has(0, True))
    for b in (B - 2, B - 1, B, B + 1):
        body(b, b % 2, has(b))


def attn_pe(nc, pe, s, g, f, w):
    mm, tr = nc.tensor.matmul, nc.tensor.transpose
    probs_full = s.p_ready if f.null else s.p_raw

    def transpose_x(b, bank):
        pe.wait_ge(s.xn_ready, b + 1)
        for t in range(ST):
            i = tr(bank[:, t * P:(t + 1) * P], w.xn[:, t, :], g.ident[:, :])
        i.then_inc(s.xT_psum, 1)

    def project(b, t, bank):
        pe.wait_ge(s.xT_ready, b + 1)
        mm(bank[:, 0:3 * D], w.xT[:, t * P:(t + 1) * P], f.wqkv[:, :], start=True, stop=True).then_inc(s.proj_psum, 1)

    def transpose_qk(b, par, n, bank):
        jp, qk = n // 2, 1 - n % 2
        pe.wait_ge(s.stage_ready, b + 1)
        pe.wait_ge(s.lo_staged, b + 1)
        src = w.k_stage if qk else w.q_stage[par]
        for jj in range(2):
            for t in range(ST):
                at = jj * T + t * P
                i = tr(bank[:, at:at + P], stage_set(src, t, 2 * jp + jj), g.ident[:, :])
        i.then_inc(s.kq_psum, 1)

    def stage_set(src, t, j):
        return src[:, t, j * HPS:(j + 1) * HPS, :].rearrange("p h r -> p (h r)")

    def transpose_max(b, par, j, bank):
        pe.wait_ge(s.slots_ready, SETS * b + j + 1)
        for t in range(ST):
            i = tr(bank[:, t * P:(t + 1) * P], stage_set(w.q_stage[par], t, j), g.ident[:, :])
        i.then_inc(s.max_psum, 1)

    def pass1(b, par, n, first):
        for hh in range(2):
            j, r = divmod(2 * n + hh, HPS)
            rows = slice(SLOT * r, SLOT * r + KQ)
            if not (first and n == 0):
                pe.wait_ge(s.s1_read, 2 * (PAIRS * b + n - 1) + hh + 1)
            o = w.s1[hh]
            mm(o[:, 0:P], w.qT[rows, par, j, 0:P], w.kT[rows, par, j, 0:P], start=True, stop=True)
            mm(o[:, P:HC], w.qT[rows, par, j, P:T], w.kT[rows, par, j, 0:T], start=True, stop=True).then_inc(s.s1_full, 1)

    def pass2(b, par, n, first):
        done = PAIRS * b + n
        if n % 2 == 0:
            pe.wait_ge(s.q2_ready, SETS * b + n // 2 + 1)
        if not (first and n == 0):
            pe.wait_ge(s.p_raw if f.null else s.s2_biased, done)
        for hh in range(2):
            j, r = divmod(2 * n + hh, HPS)
            rows = slice(SLOT * r, SLOT * r + KQ + 2)
            o = w.s2[hh]
            mm(o[:, 0:T], w.kT[rows, par, j, 0:P], w.q2T[rows, j, 0:T], start=True, stop=True)
            i = mm(o[:, T:HC], w.kT[rows, par, j, P:T], w.q2T[rows, j, P:T], start=True, stop=True)
        i.then_inc(s.s2_full, 1)

    def values(b, par, n):
        if n == 0:
            pe.wait_ge(s.values_ready, b + 1)
        if n in (0, PAIRS // 2):
            reached(pe, s.o_copied, 2 * b + n // (PAIRS // 2))
        pe.wait_ge(probs_full, PAIRS * b + n + 1)
        for hh in range(2):
            h = 2 * n + hh
            j, r = divmod(h, HPS)
            o = w.o[SLOT * r:SLOT * r + w.VC, :]
            at = (j % 2) * T
            pr = w.probs[:, n % w.NPR, hh, :]
            mm(o[:, at:at + T], w.v[:, par, 0, h, :], pr[:, 0:T], start=True, stop=False)
            i = mm(o[:, at + P:at + T], w.v[:, par, 1, h, :], pr[:, T:HC], start=False, stop=True)
        i.then_inc(s.pv_done, 1)

    def transpose_o(b, t, bank):
        pe.wait_ge(s.o_copied, 2 * b + 2)
        for j in range(SETS):
            i = tr(bank[:, j * P:(j + 1) * P], w.oT[:, j, t * P:(t + 1) * P], g.ident[:, :])
        i.then_inc(s.ob_psum, 1)

    def transpose_att(b, bank):
        pe.wait_ge(s.att_ready, b + 1)
        for t in range(ST):
            i = tr(bank[:, t * P:(t + 1) * P], w.att[:, t, :], g.ident[:, :])
        i.then_inc(s.aT_psum, 1)

    def output(b, bank):
        pe.wait_ge(s.aT_ready, b + 1)
        for t in range(ST):
            i = mm(bank[:, t * D:(t + 1) * D], w.aT[:, t * P:(t + 1) * P], f.wo[:, :], start=True, stop=True)
        i.then_inc(s.y_psum, 1)

    m0, m1, m2 = w.misc

    def main(b, par, has):
        q = 1 - par
        for n in range(PAIRS):
            if n < P2 and has.prev:
                pass2(b - 1, q, n + PAIRS - P2, False)
            if n >= P2 and has.cur:
                pass2(b, par, n - P2, not has.ever)
            if has.cur:
                if n == 0:
                    pe.wait_ge(s.kq_act, 2 * b + 1)
                    pe.wait_ge(s.kq_dve, 2 * b + 1)
                if n == PAIRS // 2:
                    pe.wait_ge(s.kq_act, 2 * b + 2)
                    pe.wait_ge(s.kq_dve, 2 * b + 2)
                pass1(b, par, n, not has.ever)
            if n < PV and has.prev:
                values(b - 1, q, n + PAIRS - PV)
            if n >= PV and has.cur:
                values(b, par, n - PV)
            if n == 0 and has.prev:
                if has.cur:
                    pe.wait_ge(s.kq_act, 2 * b + 2)
                transpose_max(b - 1, q, SETS - 1, m0)
            if n == 0 and has.prev2:
                if has.cur:
                    pe.wait_ge(s.kq_dve, 2 * b + 2)
                reached(pe, s.att_ready, b - 1)
                output(b - 2, m1)
            if n == 2 and has.cur:
                pe.wait_ge(s.kq_dve, 2 * b + 1)
                reached(pe, s.aT_ready, b - 1)
                transpose_max(b, par, 0, m2)
            if n == 2 and has.nxt:
                pe.wait_ge(s.kq_act, 2 * b + 2)
                reached(pe, s.q2_ready, SETS * b)
                transpose_x(b + 1, m0)
            if n == 3 and has.nxt:
                pe.wait_ge(s.kq_dve, 2 * b + 2)
                reached(pe, s.x_done, b - 1)
                project(b + 1, 0, m1)
                pe.wait_ge(s.q2_ready, SETS * b + 1)
                project(b + 1, 1, m2)
            if n == 4 and has.cur:
                if has.nxt:
                    pe.wait_ge(s.xT_ready, b + 2)
                reached(pe, s.q2_ready, SETS * b)
                transpose_max(b, par, 1, m0)
            if n == 5 and has.prev:
                if has.nxt:
                    pe.wait_ge(s.proj_read, b + 2)
                if has.cur:
                    pe.wait_ge(s.q2_ready, SETS * b + 1)
                reached(pe, s.x_done, b - 1)
                reached(pe, s.aT_ready, b - 1)
                transpose_o(b - 1, 0, m1)
                transpose_o(b - 1, 1, m2)
            if n == 6 and has.cur:
                pe.wait_ge(s.q2_ready, SETS * b + 2)
                transpose_max(b, par, 2, m0)
            if n == 7 and has.nxt:
                if has.prev:
                    pe.wait_ge(s.att_ready, b)
                pe.wait_ge(s.proj_read, b + 2)
                transpose_qk(b + 1, q, 0, m1)
                transpose_qk(b + 1, q, 1, m2)
                pe.wait_ge(s.q2_ready, SETS * b + 3)
                transpose_qk(b + 1, q, 2, m0)
                pe.wait_ge(s.kq_act, 2 * b + 3)
                transpose_qk(b + 1, q, 3, m1)
            if n == 7 and has.prev:
                if has.nxt:
                    pe.wait_ge(s.kq_dve, 2 * b + 3)
                transpose_att(b - 1, m2)

    pe.wait_ge(s.o_clear, 1)
    transpose_x(0, m0)
    project(0, 0, m1)
    project(0, 1, m2)
    pe.wait_ge(s.proj_read, 1)
    transpose_qk(0, 0, 0, m1)
    transpose_qk(0, 0, 1, m2)
    transpose_qk(0, 0, 2, m0)
    pe.wait_ge(s.kq_act, 1)
    transpose_qk(0, 0, 3, m1)
    over_sequences(pe, main)


def heads(x):
    return x.rearrange("p t (h d) -> p t h d", d=HD)


def part(x, n):
    return x[:, :, :, n * HD:(n + 1) * HD]


def attn_act(nc, act, s, g, f, w):
    m0, m1, m2 = w.misc

    def stage_hi(b, par):
        act.wait_ge(s.proj_read, b + 1)
        reached(act, s.max_psum, SETS * (b - 1))
        reached(act, s.kq_psum, 4 * b)
        q, k = heads(w.qkv[:, :, 0:D]), heads(w.qkv[:, :, D:2 * D])
        nc.scalar.copy(part(w.k_stage, 0).bitcast(fp32r), k)
        nc.scalar.copy(part(w.q_stage[par], 0).bitcast(fp32r), q).then_inc(s.hi_staged, 1)
        nc.scalar.copy(part(w.k_stage, 1).bitcast(fp32r), k)
        nc.scalar.copy(part(w.q_stage[par], 2).bitcast(fp32r), q).then_inc(s.stage_ready, 1)

    def place_values(b, par):
        reached(act, s.pv_done, PAIRS * (b - 1))
        nc.scalar.copy(w.v[:, par, :, :, 0:HD], heads(w.qkv[:, :, 2 * D:3 * D])).then_inc(s.values_ready, 1)

    def copy_xT(b):
        act.wait_ge(s.xT_psum, b + 1)
        reached(act, s.proj_psum, 2 * b)
        nc.scalar.copy(w.xT[:, :], m0[:, 0:T]).then_inc(s.xT_ready, 1)

    def copy_kq(b, par, n, bank):
        act.wait_ge(s.kq_psum, 4 * b + n + 1)
        reached(act, s.s2_full, PAIRS * (b - 1))
        nc.scalar.copy(w.kT[:, par, n:n + 2, :], bank[:, :].rearrange("p (j t) -> p j t", t=T)).then_inc(s.kq_act, 1)

    def copy_q2(b, j, bank):
        act.wait_ge(s.max_psum, SETS * b + j + 1)
        reached(act, s.s2_full, PAIRS * (b - 1) + 2 * j + 2)
        nc.scalar.copy(w.q2T[:, j, :], bank[:, 0:T]).then_inc(s.q2_ready, 1)

    def exponential(b, n, first):
        if f.null:
            act.wait_ge(s.s2_full, PAIRS * b + n + 1)
        else:
            act.wait_ge(s.s2_biased, PAIRS * b + n + 1)
        if not (first and n < w.NPR):
            act.wait_ge(s.pv_done, PAIRS * b + n + 1 - w.NPR)
        src = w.s2_pair if f.null else w.biased[:, n % w.NB, :, :]
        nc.scalar.activation(w.probs[:, n % w.NPR, :, :], src, ACT.Exp).then_inc(s.p_raw, 1)

    def copy_o(b, half):
        act.wait_ge(s.pv_done, PAIRS * b + (half + 1) * PAIRS // 2)
        reached(act, s.ob_psum, 2 * b)
        nc.scalar.copy(w.oT[:, 2 * half:2 * half + 2, :], w.o[:, :].rearrange("p (j t) -> p j t", t=T)).then_inc(s.o_copied, 1)

    def copy_aT(b):
        act.wait_ge(s.aT_psum, b + 1)
        reached(act, s.y_psum, b)
        nc.scalar.copy(w.aT[:, :], m2[:, 0:T]).then_inc(s.aT_ready, 1)

    def main(b, par, has):
        for n in range(PAIRS):
            if n < P2 and has.prev:
                exponential(b - 1, n + PAIRS - P2, False)
            if n >= P2 and has.cur:
                exponential(b, n - P2, not has.ever)
            if n == 0 and has.prev:
                copy_q2(b - 1, SETS - 1, m0)
                copy_o(b - 1, 0)
                if f.null:
                    act.wait_ge(s.null_in, b)
                    reached(act, s.att_ready, b - 1)
                    nc.scalar.activation(w.null_p[:, :], w.null_d[:, :], ACT.Exp).then_inc(s.null_exp, 1)
            if n == 2 and has.cur:
                copy_q2(b, 0, m2)
            if n == 2 and has.nxt:
                copy_xT(b + 1)
            if n == 4 and has.prev:
                copy_o(b - 1, 1)
            if n == 4 and has.cur:
                copy_q2(b, 1, m0)
            if n == 6 and has.cur:
                copy_q2(b, 2, m0)
            if n == 5 and has.nxt:
                stage_hi(b + 1, 1 - par)
                place_values(b + 1, 1 - par)
            if n == 7 and has.nxt:
                copy_kq(b + 1, 1 - par, 0, m1)
                copy_kq(b + 1, 1 - par, 2, m0)
            if n == 7 and has.prev:
                copy_aT(b - 1)

    act.wait_ge(s.slots_clear, 1)
    copy_xT(0)
    stage_hi(0, 0)
    place_values(0, 0)
    copy_kq(0, 0, 0, m1)
    copy_kq(0, 0, 2, m0)
    over_sequences(act, main)


def attn_pool(nc, pool, s, g, f, w, x_before):
    v = nc.gpsimd

    def rstd(b):
        pool.wait_ge(s.stats_ready, b + 1)
        reached(pool, s.xn_ready, b)
        v.tensor_tensor(w.vare[:, :], w.mv[:, :, 1], g.eps[:, 0:ST], ALU.add).then_inc(s.pool_link, 1)
        pool.wait_ge(s.pool_link, b + 1)
        v.tensor_tensor(w.rstd[:, :], w.vare[:, :], g.neg_half[:, 0:ST], ALU.pow).then_inc(s.rstd_ready, 1)

    def carry(n):
        v.tensor_tensor(w.carrier[:, n:n + 1], g.eps[:, 0:1], g.eps[:, 0:1], ALU.mult)

    def null_products(b):
        pool.wait_ge(s.proj_read, b + 1)
        reached(pool, s.null_score, b)
        v.tensor_tensor(w.null_qk[:, :, :], w.qkv[:, :, 0:D], f.k_null[:, :].unsqueeze(1).broadcast_to([P, ST, D]),
                        ALU.mult).then_inc(s.null_prod, 1)

    def keep(b, n):
        reached(pool, s.p_ready, PAIRS * b + n)
        pool.wait_ge(s.p_raw, PAIRS * b + n + 1)
        carry(0)
        pr = w.probs[:, n % w.NPR, :, :]
        for at in (0, T):
            d = pr[:, :, at:at + P]
            i = v.affine_select(out=d, in_=d, pattern=[[0, 2], [1, P]], compare_op=ALU.is_ge, fill=0.0, base=0,
                                channel_multiplier=-1)
        i.then_inc(s.p_ready, 1)

    def null_values(b):
        pool.wait_ge(s.null_exp, b + 1)
        reached(pool, s.att_ready, b)
        v.tensor_tensor(w.nulls[:, :, :, :], f.v_null[:, :].rearrange("p (h d) -> p h d", d=HD).unsqueeze(1).broadcast_to([P, ST, H, HD]),
                        w.null_p[:, :].rearrange("p (t h) -> p t h", h=H).unsqueeze(3).broadcast_to([P, ST, H, HD]),
                        ALU.mult).then_inc(s.nulls_ready, 1)

    def add_output_bias(b):
        pool.wait_ge(s.xn_ready, b + 1)
        rows = tiles(g.x, b, ST)
        v.tensor_tensor(rows, rows, f.bo[:, :].unsqueeze(1).broadcast_to([P, ST, D]), ALU.add).then_inc(s.rows_biased, 1)

    def main(b, par, has):
        for n in range(PAIRS):
            if not f.null and n == 3 and has.nxt:
                add_output_bias(b + 1)
            if f.null:
                if n < P2 and has.prev:
                    keep(b - 1, n + PAIRS - P2)
                if n >= P2 and has.cur:
                    keep(b, n - P2)
                if n == 1 and has.prev:
                    null_values(b - 1)
            if n == 0 and has.nxt:
                rstd(b + 1)
            if n == 4 and f.null and has.nxt:
                null_products(b + 1)

    x_before(pool)
    v.memset(w.k_stage[:, :, :, KQ:KQ + 2], 1.0)
    v.memset(w.k_stage[:, :, :, KQ + 2:SLOT], 0.0)
    for qs in w.q_stage:
        v.memset(qs[:, :, :, KQ:SLOT], 0.0)
    v.memset(w.v[:, :, :, :, HD:HD + 1], 1.0)
    v.memset(w.v[:, :, :, :, HD + 1:], 0.0).then_inc(s.slots_clear, 1)
    rstd(0)
    if f.null:
        null_products(0)
    if not f.null:
        add_output_bias(0)
    over_sequences(pool, main)


def attn_dve(nc, dve, s, g, f, w, x_before):
    v = nc.vector
    m0, m1, m2 = w.misc

    def row(b, t):
        return g.x[:, bass.ds(b * ST + t, 1), :][:, 0, :]

    def stats(b):
        reached(dve, s.rstd_ready, b)
        for t in range(ST):
            i = v.bn_stats(w.bn[:, t, :], row(b, t))
        i.then_inc(s.stats_step, 1)

    def aggregate(b):
        for t in range(ST):
            i = v.bn_aggr(w.mv[:, t, :], w.bn[:, t, :])
        i.then_inc(s.stats_ready, 1)

    def norm(b):
        dve.wait_ge(s.rstd_ready, b + 1)
        dve.wait_ge(s.stats_ready, b + 1)
        reached(dve, s.xT_psum, b)
        for t in range(ST):
            i = v.tensor_scalar(w.xn[:, t, :], row(b, t), w.mv[:, t, 0:1], w.rstd[:, t:t + 1], ALU.subtract, ALU.mult)
        i.then_inc(s.xn_ready, 1)

    def read_projections(b):
        reached(dve, s.stage_ready, b)
        reached(dve, s.values_ready, b)
        if f.null:
            reached(dve, s.null_prod, b)
        for t, bank in enumerate((m1, m2)):
            dve.wait_ge(s.proj_psum, ST * b + t + 1)
            if f.null:
                v.tensor_tensor(w.qkv[:, t, 0:2 * D], bank[:, 0:2 * D], f.cos[:, t, :], ALU.mult)
                heads2 = bank[:, 0:2 * D].rearrange("p (h d) -> p h d", d=HD)
                v.tensor_tensor(w.turned[:, t, :, 0:2], heads2[:, :, 6:8], f.sin[:, t, :, 0:2], ALU.mult)
                v.tensor_tensor(w.turned[:, t, :, 2:4], heads2[:, :, 4:6], f.sin[:, t, :, 2:4], ALU.mult)
                i = v.tensor_copy(w.qkv[:, t, 2 * D:3 * D], bank[:, 2 * D:3 * D])
            else:
                i = v.tensor_tensor(w.qkv[:, t, :], bank[:, 0:3 * D], f.bqkv[:, :], ALU.add)
        if f.null:
            i.then_inc(s.proj_step, 1)
            dve.wait_ge(s.proj_step, b + 1)
            for t in range(ST):
                geo = w.qkv[:, t, 0:2 * D].rearrange("p (h d) -> p h d", d=HD)[:, :, 4:8]
                i = v.tensor_tensor(geo, geo, w.turned[:, t, :, :], ALU.add)
        i.then_inc(s.proj_read, 1)

    def stage_lo(b, par):
        dve.wait_ge(s.hi_staged, b + 1)
        for x, hi, lo, at in ((w.qkv[:, :, 0:D], w.q_stage[par], w.q_stage[par], 1), (w.qkv[:, :, D:2 * D], w.k_stage, w.k_stage, 2)):
            i = v.tensor_tensor(part(lo, at).bitcast(fp32r), heads(x), part(hi, 0), ALU.subtract)
        i.then_inc(s.lo_staged, 1)

    def null_scores(b, par):
        dve.wait_ge(s.null_prod, b + 1)
        v.tensor_reduce(w.null_s[:, par, :], w.null_qk[:, :, :].rearrange("p t (h d) -> p (t h) d", d=HD), AX.X,
                        ALU.add).then_inc(s.null_score, 1)

    def copy_kq(b, par, n, bank):
        dve.wait_ge(s.kq_psum, 4 * b + n + 1)
        reached(dve, s.s1_full, H * (b - 1))
        v.tensor_copy(w.qT[:, par, n - 1:n + 1, :], bank[:, :].rearrange("p (j t) -> p j t", t=T)).then_inc(s.kq_dve, 1)

    def maxima(b, par, n):
        if f.null and n == 0:
            dve.wait_ge(s.null_score, b + 1)
        dve.wait_ge(s.s1_full, H * b + 2 * n + 2)
        v.tensor_copy(w.dve_carrier[:, :], g.eps[:, 0:1])
        for hh in range(2):
            h = 2 * n + hh
            for t, (lo, hi) in enumerate(((0, P), (P, HC))):
                least = w.null_s[:, par, t * H + h:t * H + h + 1] if f.null else LEAST
                i = v.tensor_tensor_reduce(out=w.junk[:, hh, lo:hi], in0=w.s1[hh][:, lo:hi], in1=f.bias_q(h, t), scale=1.0,
                                           scalar=least, op0=ALU.add, op1=ALU.max, accum_out=w.top[:, t, h:h + 1])
            i.then_inc(s.s1_read, 1)

    def place_maxima(b, par, j):
        dve.wait_ge(s.s1_read, H * b + (j + 1) * HPS)
        dve.wait_ge(s.kq_psum, 4 * b + 4)
        top = w.top[:, :, j * HPS:(j + 1) * HPS].unsqueeze(3)
        at = w.q_stage[par][:, :, j * HPS:(j + 1) * HPS, :]
        v.tensor_scalar(at[:, :, :, KQ:KQ + 1].bitcast(fp32r), top, -1.0, None, ALU.mult).then_inc(s.slot_step, 1)
        dve.wait_ge(s.slot_step, SETS * b + j + 1)
        v.scalar_tensor_tensor(out=at[:, :, :, KQ + 1:KQ + 2].bitcast(fp32r), in0=top, scalar=-1.0,
                               in1=at[:, :, :, KQ:KQ + 1], op0=ALU.mult, op1=ALU.subtract).then_inc(s.slots_ready, 1)

    def add_bias(b, n, first):
        dve.wait_ge(s.s2_full, PAIRS * b + n + 1)
        if not (first and n < w.NB):
            dve.wait_ge(s.p_raw, PAIRS * b + n + 1 - w.NB)
        v.tensor_tensor(w.biased[:, n % w.NB, :, 0:T], w.s2_pair[:, :, 0:T], f.bias_k(2 * n, T), ALU.add)
        v.tensor_tensor(w.biased[:, n % w.NB, :, T:HC], w.s2_pair[:, :, T:HC], f.bias_k(2 * n, P), ALU.add).then_inc(s.s2_biased, 1)

    def finish(b):
        reached(dve, s.aT_psum, b)
        if f.null:
            dve.wait_ge(s.nulls_ready, b + 1)
        for t, bank in enumerate((m1, m2)):
            dve.wait_ge(s.ob_psum, 2 * b + t + 1)
            sums = bank[:, :].rearrange("p (h d) -> p h d", d=SLOT)
            if f.null:
                v.tensor_tensor(w.den[:, t, :], sums[:, :, HD], w.null_p[:, t * H:(t + 1) * H], ALU.add)
                i = v.tensor_tensor(w.num[:, t, :, :], sums[:, :, 0:HD], w.nulls[:, t, :, :], ALU.add)
            else:
                v.tensor_copy(w.den[:, t, :], sums[:, :, HD])
                i = v.tensor_copy(w.num[:, t, :, :], sums[:, :, 0:HD])
        i.then_inc(s.fin_step, 1)
        dve.wait_ge(s.fin_step, 2 * b + 1)
        v.reciprocal(w.rden[:, :, :], w.den[:, :, :]).then_inc(s.fin_step, 1)
        dve.wait_ge(s.fin_step, 2 * b + 2)
        v.tensor_tensor(w.att[:, :, :].rearrange("p t (h d) -> p (t h) d", d=HD), w.num[:, :, :, :].rearrange("p t h d -> p (t h) d"),
                        w.rden[:, :, :].rearrange("p t h -> p (t h)").unsqueeze(2).broadcast_to([P, ST * H, HD]),
                        ALU.mult).then_inc(s.att_ready, 1)

    def update(b):
        dve.wait_ge(s.y_psum, b + 1)
        if not f.null:
            dve.wait_ge(s.rows_biased, b + 1)
        rows = tiles(g.x, b, ST)
        v.tensor_tensor(rows, m1[:, 0:T].rearrange("p (t d) -> p t d", d=D), rows, ALU.add).then_inc(s.x_done, 1)

    def main(b, par, has):
        for n in range(PAIRS):
            if n == 0 and f.null and has.prev:
                dve.wait_ge(s.s1_read, H * b)
                reached(dve, s.null_exp, b - 1)
                v.tensor_tensor(w.null_d[:, :], w.null_s[:, 1 - par, :], w.top[:, :, :].rearrange("p t h -> p (t h)"),
                                ALU.subtract).then_inc(s.null_in, 1)
                dve.wait_ge(s.null_in, b)
            if not f.null:
                if n < P2 and has.prev:
                    add_bias(b - 1, n + PAIRS - P2, False)
                if n >= P2 and has.cur:
                    add_bias(b, n - P2, not has.ever)
            if n == 0 and has.nxt:
                stats(b + 1)
            if n == 0 and has.nxt:
                dve.wait_ge(s.stats_step, b + 2)
            if has.cur:
                maxima(b, par, n)
                if n % 2:
                    place_maxima(b, par, n // 2)
            if n == 0 and has.nxt:
                aggregate(b + 1)
            if n == 1 and has.prev2:
                update(b - 2)
            if n == 1 and has.nxt:
                norm(b + 1)
            if n == 3 and has.nxt:
                read_projections(b + 1)
            if n == 6 and has.nxt:
                stage_lo(b + 1, 1 - par)
            if n == 5 and f.null and has.nxt:
                null_scores(b + 1, 1 - par)
            if n == 5 and has.prev:
                finish(b - 1)
            if n == 7 and has.nxt:
                copy_kq(b + 1, 1 - par, 1, m2)
                copy_kq(b + 1, 1 - par, 3, m1)

    x_before(dve)
    v.memset(w.o[:, :], 0.0).then_inc(s.o_clear, 1)
    stats(0)
    dve.wait_ge(s.stats_step, 1)
    aggregate(0)
    norm(0)
    read_projections(0)
    stage_lo(0, 0)
    if f.null:
        null_scores(0, 0)
    copy_kq(0, 0, 1, m2)
    copy_kq(0, 0, 3, m1)
    over_sequences(dve, main)


def program(nc, a, out, stages=("ffn0", "attn0", "ffn0", "ffn1", "attn1", "ffn1")):
    ctx = ExitStack()
    with ctx:
        def sb(name, shape, dt=fp32, stack=ctx):
            return stack.enter_context(nc.sbuf_tensor(name, shape, dt))

        def sem(name):
            return ctx.enter_context(nc.semaphore(name))

        pair = ctx.enter_context(nc.psum_tensor("bank_pair", [P, 2, 512], fp32))
        banks = [ctx.enter_context(nc.psum_tensor(f"bank{i}", [P, 512], fp32)) for i in range(6)]
        banks[2:2] = [pair[:, 0, :], pair[:, 1, :]]

        g = group(
            x=sb("x", [P, B * T // P, D]), ident=sb("ident", [P, P]), ident_bf=sb("ident_bf", [P, P], bf16),
            pick=sb("pick", [WR, E, P], bf16), lower=sb("lower", [P, E * E]),
            neg_half=sb("neg_half", [P, CT]), eps=sb("eps", [P, CT]))

        def ffn_weights(name, nb, stack=ctx):
            n = E * nb
            return dict(nb=nb, up_hi=sb(f"{name}_up_hi", [P, n, P], fp32r, stack), up_lo=sb(f"{name}_up_lo", [P, n, P], fp32r, stack),
                        down=sb(f"{name}_down", [P, n, D], fp32, stack), gate=sb(f"{name}_gate", [P, E], fp32, stack))

        f1 = group(**ffn_weights("ffn1", 4), sigmoid=False, square=False, b1=sb("b1", [P, 4 * E]),
                             b2=sb("b2_split", [WR, D], bf16), scale=0.5 / E)
        mask = sb("mask", [P, T])
        a0 = group(null=True, wqkv=sb("wqkv0", [P, 3 * D]), wo=sb("wo0", [P, D]), k_null=sb("k_null", [P, D]),
                   v_null=sb("v_null", [P, D]), cos=sb("cos", [P, ST, 2 * D]), sin=sb("sin", [P, ST, 2 * H, HD // 2]),
                   bias_q=lambda h, t: mask[:, :] if t else mask[:, P:T])
        with ExitStack() as own:
            f0 = group(**ffn_weights("ffn0", 2, own), sigmoid=True, square=True, b1=None, b2=None, scale=0.5,
                                 expert_bias=sb("expert_bias", [P, E], fp32, own))
        table_k = sb("table_k", [P, H, T])
        table_q = sb("table_q", [P, H, T])
        a1 = group(null=False, wqkv=sb("wqkv1", [P, 3 * D]), wo=sb("wo1", [P, D]), bqkv=sb("bqkv", [P, 3 * D]),
                   bo=sb("bo", [P, D]), bias_q=lambda h, t: table_q[:, h, :] if t else table_q[:, h, P:T],
                   bias_k=lambda h, n: table_k[:, h:h + 2, 0:n])

        stack = ExitStack()

        def fb(name, shape, dt=fp32):
            return sb(name, shape, dt, stack)

        m = Buffers()
        m.NU, m.NR, m.NS, m.NH = 4, 4, 4, 4
        m.up, m.wb, m.y, m.misc = banks[0:4], banks[4:6], banks[6], banks[7]
        m.misc_bf = m.misc[:, :].bitcast(bf16)
        m.bn, m.mv = fb("bn", [P, CT, 6]), fb("mv", [P, CT, 2])
        m.vare, m.rstd = fb("vare", [P, CT]), fb("rstd", [P, CT])
        m.xn, m.xT = fb("xn", [P, CT, D]), fb("xT", [P, CW])
        m.x_hi, m.x_lo = fb("x_hi", [P, 2, CW], fp32r), fb("x_lo", [P, 2, CW], fp32r)
        m.gexp, m.gsub, m.glog = fb("gexp", [P, CT * E]), fb("gsub", [P, CT * E]), fb("glog", [P, CT, E])
        m.glog_flat = m.glog[:, :, :].rearrange("p t e -> p (t e)")
        m.gmax, m.chosen, m.biased = fb("gmax", [P, CT, 8]), fb("chosen", [P, CT, E]), fb("biased", [P, CT, E])
        m.ahead, m.tied = fb("ahead", [P, CT, E, E]), fb("tied", [P, CT, E, E])
        m.rank, m.w = fb("rank", [P, CT, E]), fb("w", [P, CT, E])
        m.wsum, m.wrec = fb("wsum", [P, CT]), fb("wrec", [P, CT])
        m.wparts = fb("wparts", [P, CT, NPARTS, NPARTS, E], bf16)
        m.wparts_flat = m.wparts[:, :, :, :, :].rearrange("p t b a e -> p t (b a e)")
        m.wT = fb("wT", [WR, 2, CW], bf16)
        m.relu, m.scaled, m.h = fb("relu", [P, m.NR, CW]), fb("scaled", [P, m.NS, CW]), fb("h", [P, m.NH, CW])
        m.yT = fb("yT", [P, CW])
        up0, up1 = fb("up0", [P, 2 * E, P]), fb("up1", [P, 4 * E, P])
        pick_f, part_rows = fb("pick_f", [WR, E, P]), fb("part_rows", [WR, NPARTS])
        b2_rows, b2_part, b2_sum = fb("b2_rows", [WR, D]), fb("b2_part", [WR, D], bf16), fb("b2_sum", [WR, D])
        rel, flip, distance = fb("rel", [P, D]), fb("flip", [P, P]), fb("distance", [P, H])
        curves = fb("curves", [H, 4, T])
        curves_dram = nc.dram_tensor("curves_dram", (H, 4, P, T), fp32, kind="Internal")
        stack.close()

        stack = ExitStack()
        w = Buffers()
        w.VC, w.NPR, w.NB = 2 * HD, 2, 1
        w.s1, w.s2, w.o, w.misc, w.s2_pair = banks[0:2], banks[2:4], banks[4], banks[5:8], pair[:, :, 0:HC]
        w.bn, w.mv = fb("abn", [P, ST, 6]), fb("amv", [P, ST, 2])
        w.vare, w.rstd = fb("avare", [P, ST]), fb("arstd", [P, ST])
        w.xn, w.xT, w.qkv = fb("axn", [P, ST, D]), fb("axT", [P, T]), fb("qkv", [P, ST, 3 * D])
        w.turned = fb("turned", [P, ST, 2 * H, HD // 2])
        w.q_stage = [fb(f"q_stage{i}", [P, ST, H, SLOT]) for i in range(2)]
        w.k_stage = fb("k_stage", [P, ST, H, SLOT])
        w.qT, w.kT = fb("qT", [P, 2, SETS, T], fp32r), fb("kT", [P, 2, SETS, T], fp32r)
        w.q2T = fb("q2T", [P, SETS, T], fp32r)
        w.v = fb("v", [P, 2, ST, H, w.VC])
        w.junk, w.top = fb("junk", [P, 2, HC]), fb("top", [P, ST, H])
        w.null_qk, w.null_s = fb("null_qk", [P, ST, D]), fb("null_s", [P, 2, ST * H])
        w.null_d, w.null_p = fb("null_d", [P, ST * H]), fb("null_p", [P, ST * H])
        w.nulls, w.num = fb("nulls", [P, ST, H, HD]), fb("num", [P, ST, H, HD])
        w.den, w.rden = fb("den", [P, ST, H]), fb("rden", [P, ST, H])
        w.biased = fb("biased_scores", [P, w.NB, 2, HC])
        w.probs = fb("probs", [P, w.NPR, 2, HC])
        w.carrier, w.dve_carrier = fb("carrier", [P, 3]), fb("dve_carrier", [P, 1])
        w.oT, w.att, w.aT = fb("oT", [P, SETS, T]), fb("att", [P, ST, D]), fb("aT", [P, T])
        stack.close()

        load_x, load_const, load_ffn0, load_ffn1, load_attn, load_tables = (
            sem(n) for n in "load_x load_const load_ffn0 load_ffn1 load_attn load_tables".split())
        const_ready, b2_step, up0_hi, up0_lo, up1_hi, up1_lo = (
            sem(n) for n in "const_ready b2_step up0_hi up0_lo up1_hi up1_lo".split())
        distance_sum, curve_psum, curves_ready, curves_stored, scaled_qkv, stored = (
            sem(n) for n in "distance_sum curve_psum curves_ready curves_stored scaled_qkv stored".split())

        layer_kinds = ("ffn0", "ffn1")
        unused = {"ffn0": "gate_in", "ffn1": "h_full", "attn0": "rows_biased s2_biased",
                  "attn1": "null_prod null_score null_in null_exp nulls_ready p_ready proj_step"}
        sems = {kind: group(**{x: sem(f"{kind}_{x}") for x in (FFN_SEMS if kind in ("ffn0", "ffn1") else ATTN_SEMS).split()
                                         if x not in unused[kind].split()}) for kind in dict.fromkeys(stages)}
        plan = [(kind, sems[kind], stages[:n].count(kind) * (NCH if kind in layer_kinds else B)) for n, kind in enumerate(stages)]
        layer = {"ffn0": f0, "ffn1": f1}
        attn = {"attn0": a0, "attn1": a1}
        split_up1 = group(raw=up1, hi=f1.up_hi, lo=f1.up_lo, hi_done=up1_hi, lo_done=up1_lo, loaded=load_ffn1)

        def after_stage(n):
            if n <= 0:
                return lambda eng: eng.wait_ge(load_x, 32)
            kind, s, c0 = plan[n - 1]
            return lambda eng: eng.wait_ge(s.x_done, c0 + (NCH if kind in layer_kinds else B))

        x_rows = a["x"].rearrange("(t p) d -> p t d", p=P)
        out_rows = out.rearrange("(t p) d -> p t d", p=P)

        def matrices(name, cols):
            return a[name].rearrange("p (n m) -> p n m", m=cols)

        constants = ((g.ident, "ident"), (g.neg_half, "neg_half"), (g.eps, "eps"), (f0.gate, "gate0"), (g.lower, "lower"),
                     (f0.expert_bias, "expert_bias"), (pick_f, "pick"), (part_rows, "part_rows"), (b2_rows, "b2"),
                     (f1.b1, "b1"), (f1.gate, "gate1"), (flip, "flip"), (rel, "rel"))
        for_attention = ((a0.wqkv, "wqkv0"), (a0.wo, "wo0"), (a0.k_null, "k_null"), (a0.v_null, "v_null"), (a0.cos, "cos"),
                         (a0.sin, "sin"), (mask, "mask"), (a1.wqkv, "wqkv1"), (a1.wo, "wo1"),
                         (a1.bqkv, "bqkv"), (a1.bo, "bo"))

        block = ctx.enter_context(nc.Block())

        @block.sync
        def _(sp):
            sp.dma_start(tiles(g.x, 0, CT), x_rows[:, 0:CT, :]).then_inc(load_x, 16)
            sp.dma_start(up0[:, :, :], matrices("up0", P)).then_inc(load_ffn0, 16)
            for dst, name in constants:
                sp.dma_start(whole(dst), a[name]).then_inc(load_const, 16)
            sp.dma_start(g.x[:, CT:, :], x_rows[:, CT:, :]).then_inc(load_x, 16)
            sp.dma_start(f0.down[:, :, :], matrices("down0", D)).then_inc(load_ffn0, 16)
            sp.dma_start(up1[:, :, :], matrices("up1", P)).then_inc(load_ffn1, 16)
            for dst, name in for_attention:
                sp.dma_start(whole(dst), a[name]).then_inc(load_attn, 16)
            sp.dma_start(f1.down[:, :, :], matrices("down1", D)).then_inc(load_ffn1, 16)
            sp.wait_ge(curves_ready, 1)
            for n in range(4):
                sp.dma_start(curves_dram[:, n, :, :], curves[:, n:n + 1, :].broadcast_to([H, P, T])).then_inc(curves_stored, 16)
            sp.wait_ge(curves_stored, 64)
            if "attn1" in stages:
                uses = [n + 1 for n, kind in enumerate(stages) if kind == "ffn0"]
                if uses:
                    after_stage(uses[-1])(sp)
                for table, first in ((table_k, 0), (table_q, 2)):
                    for kind in range(2):
                        shifted = bass.AP(curves_dram, (first + kind) * P * T + P - 1, [[T - 1, P], [4 * P * T, H], [1, P]])
                        sp.dma_start(table[:, :, kind * P:(kind + 1) * P], shifted).then_inc(load_tables, 16)
            kind, s, c0 = plan[-1]
            per = CT if kind in layer_kinds else ST
            for c in range(B * T // P // per):
                sp.wait_ge(s.x_done, c0 + c + 1)
                sp.dma_start(out_rows[:, c * per:(c + 1) * per, :], tiles(g.x, c, per)).then_inc(stored, 16)
            sp.wait_ge(stored, 16 * (B * T // P // per))

        @block.vector
        def _(dve):
            v = nc.vector
            dve.wait_ge(up0_hi, 1)
            v.tensor_tensor(f0.up_lo[:, :, :], up0[:, :, :], f0.up_hi[:, :, :].bitcast(fp32), ALU.subtract).then_inc(up0_lo, 1)
            dve.wait_ge(load_const, 16 * len(constants))
            v.tensor_copy(g.ident_bf[:, :], g.ident[:, :])
            v.tensor_copy(g.pick[:, :, :], pick_f[:, :, :]).then_inc(const_ready, 1)
            v.tensor_scalar(b2_sum[:, :], b2_rows[:, :], 0.0, None, ALU.mult)
            for n in range(NPARTS):
                v.tensor_copy(b2_part[:, :], b2_rows[:, :]).then_inc(b2_step, 1)
                dve.wait_ge(b2_step, 2 * n + 1)
                v.scalar_tensor_tensor(out=b2_sum[:, :], in0=b2_part[:, :], scalar=part_rows[:, n:n + 1], in1=b2_sum[:, :],
                                       op0=ALU.mult, op1=ALU.add)
                v.tensor_tensor(b2_rows[:, :], b2_rows[:, :], b2_part[:, :], ALU.subtract).then_inc(b2_step, 1)
                dve.wait_ge(b2_step, 2 * n + 2)
            v.tensor_copy(f1.b2[:, :], b2_sum[:, :]).then_inc(const_ready, 1)
            v.tensor_reduce(distance[:, :], rel[:, :].rearrange("p (h d) -> p h d", d=HD), AX.X, ALU.add).then_inc(distance_sum, 1)
            dve.wait_ge(curve_psum, 1)
            near, far = banks[5][0:H, 0:P], banks[5][0:H, P:2 * P]
            last = near[:, P - 1:P]
            v.memset(curves[:, 0, 0:P - 1], NEG)
            v.tensor_copy(curves[:, 0, P - 1:2 * P - 1], near)
            v.memset(curves[:, 0, 2 * P - 1:], 0.0)
            v.tensor_copy(curves[:, 1, 0:P - 1], near[:, 1:P])
            v.tensor_copy(curves[:, 1, P - 1:], last.broadcast_to([H, P + 1]))
            v.tensor_copy(curves[:, 2, 0:P + 1], last.broadcast_to([H, P + 1]))
            v.tensor_copy(curves[:, 2, P + 1:], far[:, 1:P])
            v.tensor_copy(curves[:, 3, 0:P], far)
            v.memset(curves[:, 3, P:], NEG).then_inc(curves_ready, 1)
            dve.wait_ge(load_attn, 16 * len(for_attention))
            v.tensor_scalar(a1.wqkv[:, 0:D], a1.wqkv[:, 0:D], float(HD) ** -0.5, None, ALU.mult)
            v.tensor_scalar(a1.bqkv[:, 0:D], a1.bqkv[:, 0:D], float(HD) ** -0.5, None, ALU.mult).then_inc(scaled_qkv, 1)
            for n, (kind, s, c0) in enumerate(plan):
                if kind in layer_kinds:
                    ffn_dve(nc, dve, s, g, layer[kind], m, c0, after_stage(n), None if n else split_up1)
                else:
                    if kind == "attn1":
                        dve.wait_ge(load_tables, 64)
                        dve.wait_ge(scaled_qkv, 1)
                    attn_dve(nc, dve, s, g, attn[kind], w, after_stage(n))

        @block.scalar
        def _(act):
            act.wait_ge(load_ffn0, 32)
            nc.scalar.copy(f0.up_hi[:, :, :], up0[:, :, :]).then_inc(up0_hi, 1)
            act.wait_ge(load_const, 16 * len(constants))
            for n, (kind, s, c0) in enumerate(plan):
                if kind in layer_kinds:
                    ffn_act(nc, act, s, g, layer[kind], m, c0, None if n else split_up1)
                else:
                    attn_act(nc, act, s, g, attn[kind], w)

        @block.gpsimd
        def _(pool):
            pool.wait_ge(load_const, 16 * len(constants))
            pool.wait_ge(load_attn, 16 * len(for_attention))
            for n, (kind, s, c0) in enumerate(plan):
                if kind in layer_kinds:
                    ffn_pool(nc, pool, s, g, layer[kind], m, c0)
                else:
                    attn_pool(nc, pool, s, g, attn[kind], w, after_stage(n))

        @block.tensor
        def _(pe):
            pe.wait_ge(load_const, 16 * len(constants))
            pe.wait_ge(const_ready, 2)
            pe.wait_ge(distance_sum, 1)
            nc.tensor.matmul(banks[5][0:H, 0:P], distance[:, :], g.ident[:, :], start=True, stop=True)
            nc.tensor.matmul(banks[5][0:H, P:2 * P], distance[:, :], flip[:, :], start=True, stop=True).then_inc(curve_psum, 1)
            pe.wait_ge(curves_ready, 1)
            pe.wait_ge(up0_lo, 1)
            pe.wait_ge(scaled_qkv, 1)
            for n, (kind, s, c0) in enumerate(plan):
                if kind == "ffn1":
                    pe.wait_ge(up1_lo, NCH)
                if n > 0:
                    after_stage(n)(pe)
                if kind in layer_kinds:
                    ffn_pe(nc, pe, s, g, layer[kind], m, c0)
                else:
                    attn_pe(nc, pe, s, g, attn[kind], w)


def whole(t):
    return {2: lambda: t[:, :], 3: lambda: t[:, :, :], 4: lambda: t[:, :, :, :]}[len(t.shape)]()


def layouts(i):
    def c(v):
        return np.ascontiguousarray(v)

    def rows(v):
        return c(np.broadcast_to(v.reshape(1, -1), (P, v.size)))

    def by_head(sem, geo):
        n = sem.shape[0]
        return np.concatenate([sem.reshape(n, H, -1), geo.reshape(n, H, -1)], axis=2).reshape(n, D)

    eye = np.eye(P, dtype=np.float32)
    pick = np.zeros((WR, E, P), np.float32)
    for n in range(NPARTS):
        for e in range(E):
            pick[n * E + e, e] = 1.0
    part_rows = np.zeros((WR, NPARTS), np.float32)
    for n in range(NPARTS):
        part_rows[n * NPARTS * E:(n + 1) * NPARTS * E, n] = 1.0
    h0, h1 = i["L0_ffn_w_up"].shape[1], i["L1_ffn_W1"].shape[2]

    geo_hd = i["L0_attn_wq_geo"].shape[1] // H
    scale = np.float32(1.0 / np.sqrt(geo_hd))
    inv_freq = (1.0 / np.float32(10000.0) ** (np.arange(0, geo_hd, 2, dtype=np.float32) / np.float32(geo_hd))).astype(np.float32)
    angle = (np.arange(T, dtype=np.float32)[:, None] * inv_freq[None, :]).astype(np.float32)
    cs, sn = np.cos(angle), np.sin(angle)
    cos = np.ones((T, 2, H, HD), np.float32)
    cos[..., 4:6] = cos[..., 6:8] = cs[:, None, None, :]
    sin = np.zeros((T, 2, H, HD // 2), np.float32)
    sin[..., 0:2], sin[..., 2:4] = -sn[:, None, None, :], sn[:, None, None, :]
    cos[:, 0] *= scale
    sin[:, 0] *= scale
    tiled = lambda v: c(v.reshape(ST, P, -1).transpose(1, 0, 2))
    lower = np.tril(np.ones((P, P), np.float32))
    return dict(
        x=i["L0_attn_x"].reshape(B * T, D), ident=eye, flip=c(eye[::-1]), pick=pick, part_rows=part_rows,
        lower=rows(np.tril(np.ones((E, E), np.float32), -1)),
        eps=np.full((P, CT), LN_EPS, np.float32), neg_half=np.full((P, CT), -0.5, np.float32),
        gate0=c(i["L0_ffn_gate_w"].T), expert_bias=rows(i["L0_ffn_expert_bias"]),
        up0=c(i["L0_ffn_w_up"].transpose(2, 0, 1)).reshape(D, E * h0),
        down0=c(i["L0_ffn_w_down"].transpose(0, 2, 1).reshape(E * h0 // P, P, D).transpose(1, 0, 2)).reshape(P, -1),
        gate1=i["L1_ffn_W_gate"], up1=c(i["L1_ffn_W1"].transpose(1, 0, 2)).reshape(D, E * h1),
        down1=c(i["L1_ffn_W2"].reshape(E * h1 // P, P, D).transpose(1, 0, 2)).reshape(P, -1),
        b1=c(i["L1_ffn_b1"].reshape(E * h1 // P, P).T), b2=c(np.tile(i["L1_ffn_b2"], (NPARTS * NPARTS, 1))),
        wqkv0=c(np.concatenate([by_head(i["L0_attn_wq_sem"], i["L0_attn_wq_geo"]),
                                by_head(i["L0_attn_wk_sem"], i["L0_attn_wk_geo"]), i["L0_attn_wv"]], axis=1)),
        wo0=i["L0_attn_wo"], k_null=rows(by_head(i["L0_attn_k_sem_null"][None], i["L0_attn_k_geo_null"][None])),
        v_null=rows(i["L0_attn_v_null"]), cos=tiled(cos), sin=tiled(sin).reshape(P, ST, 2 * H, HD // 2),
        mask=c(np.concatenate([np.zeros((P, P), np.float32), np.where(lower > 0, np.float32(0), np.float32(NEG))], axis=1)),
        wqkv1=c(i["L1_attn_qkv_w"].T), wo1=c(i["L1_attn_proj_w"].T), bqkv=rows(i["L1_attn_qkv_b"]), bo=rows(i["L1_attn_proj_b"]),
        rel=c(i["L1_attn_rel_pos_emb"][P - 1:]),
    )


def kernel(**inputs):
    import concourse.bacc as bacc
    from concourse.bass_utils import run_bass_kernel_spmd

    arrays = layouts({n: np.asarray(v) for n, v in inputs.items()})
    nc = bacc.Bacc("TRN2", target_bir_lowering=False, num_devices=1)
    a = {n: nc.dram_tensor(f"in_{n}", v.shape, fp32, kind="ExternalInput").ap() for n, v in arrays.items()}
    out = nc.dram_tensor("out", (B * T, D), fp32, kind="ExternalOutput").ap()
    program(nc, a, out)
    r = run_bass_kernel_spmd(nc, [{f"in_{n}": v for n, v in arrays.items()}], core_ids=[0])
    return r.results[0]["out"].reshape(B, T, D)
```

```python
from collections import namedtuple
from contextlib import ExitStack

import numpy as np

import concourse.bass as bass
from concourse import mybir

fp32 = mybir.dt.float32
fp32r = mybir.dt.float32r
bf16 = mybir.dt.bfloat16
ALU = mybir.AluOpType
ACT = mybir.ActivationFunctionType
AX = mybir.AxisListType

P = 128
D = 128
T = 256
B = 16
CT = 4
CW = CT * P
NCH = B * T // CW
E = 8
TOP_K = 2
LN_EPS = 1e-5
NPARTS = 3
WR = NPARTS * NPARTS * E

LAG = 4
HI_LAG, LO_LAG = 1, 2
AT_STATS, AT_NORM, AT_XT, AT_Y, AT_SPLIT, AT_GATE, AT_ROUTE, AT_EXP, AT_RANK, AT_WEIGHTS, AT_PARTS, AT_W = 0, 3, 5, 6, 6, 8, 8, 9, 10, 11, 12, 14
LINKS = 20


def group(**named):
    return namedtuple("Group", named)(**named)


class Buffers:
    pass


def reached(eng, sem, value):
    if not isinstance(value, int) or value > 0:
        eng.wait_ge(sem, value)


class Link:

    def __init__(self, eng, sem, chunk):
        self.eng, self.sem, self.at, self.taken = eng, sem, chunk * LINKS, 0

    def __call__(self, instruction):
        self.at, self.taken = self.at + 1, self.taken + 1
        instruction.then_inc(self.sem, 1)
        self.eng.wait_ge(self.sem, self.at)

    def close(self):
        self.eng.sem_inc(self.sem, LINKS - self.taken)


def tiles(x, c, n):
    return x[:, bass.ds(c * n, n), :]


def over_pairs(eng, body, start, count):
    body(start, 0, True, False)
    body(start + 1, 1, False, False)
    with eng.Fori(start // 2 + 1, (start + count) // 2 - 1) as i:
        body(2 * i, 0, False, False)
        body(2 * i + 1, 1, False, False)
    body(start + count - 2, 0, False, False)
    body(start + count - 1, 1, False, True)


FFN_SEMS = ("stats_step link pool_link stats_ready rstd_ready xn_ready xT_psum xT_ready xsplit_ready gate_psum gate_in gate_exp "
            "w_ready wT_psum wT_ready wb_full wb_copied up_full relu_full scaled_full h_full hi_full lo_even lo_odd down_done y_full yT_ready y_psum x_done")


def lo_ready(eng, s, f, c, k):
    eng.wait_ge(s.lo_odd if k % 2 else s.lo_even, c * (E * f.nb // 2) + k // 2 + 1)


def lagged(body, lag, nbk, c, k, first):
    if k >= lag:
        body(c, k - lag, first)
    elif not first:
        body(c - 1, k - lag + nbk, False)


def ffn_pe(nc, pe, s, g, f, m, c0, before_chunks):
    NBK = E * f.nb
    mm = nc.tensor.matmul

    def transpose_x(c):
        pe.wait_ge(s.xn_ready, c + 1)
        for t in range(CT):
            i = nc.tensor.transpose(m.misc[:, t * P:(t + 1) * P], m.xn[:, t, :], g.ident[:, :])
        i.then_inc(s.xT_psum, 1)

    def gates(c):
        pe.wait_ge(s.xT_ready, c + 1)
        for t in range(CT):
            i = mm(m.misc[:, t * E:(t + 1) * E], m.xT[:, t * P:(t + 1) * P], f.gate[:, :], start=True, stop=True)
        i.then_inc(s.gate_psum, 1)

    def transpose_w(c):
        pe.wait_ge(s.w_ready, c + 1)
        for t in range(CT):
            i = nc.tensor.transpose(m.misc_bf[0:WR, t * P:(t + 1) * P], m.wparts_flat[:, t, :], g.ident_bf[:, :])
        i.then_inc(s.wT_psum, 1)

    def transpose_y(c):
        pe.wait_ge(s.yT_ready, c + 1)
        for t in range(CT):
            i = nc.tensor.transpose(m.misc[:, t * P:(t + 1) * P], m.yT[:, t * P:(t + 1) * P], g.ident[:, :])
        i.then_inc(s.y_psum, 1)

    def down(c, par, k):
        if k == 0:
            reached(pe, s.yT_ready, c)
        pe.wait_ge(s.hi_full, c * NBK + k + 1)
        mm(m.y[:, :], f.down_hi[:, k, :], m.h_hi[:, k % m.NH, :], start=k == 0, stop=False)
        mm(m.y[:, :], f.down_lo[:, k, :], m.h_hi[:, k % m.NH, :], start=False, stop=False)
        lo_ready(pe, s, f, c, k)
        last = k == NBK - 1
        i = mm(m.y[:, :], f.down_hi[:, k, :], m.h_lo[:, k % m.NH, :], start=False, stop=last and f.b2 is None)
        i.then_inc(s.down_done, 1)
        if last and f.b2 is not None:
            mm(m.y[:, :], f.b2[0:WR, :], m.wT[0:WR, par, :], start=False, stop=True).then_inc(s.y_full, 1)

    def main(c, par, first, last):
        for k in range(NBK):
            e, hb = divmod(k, f.nb)
            if hb == 0:
                if e == 0:
                    pe.wait_ge(s.wT_ready, c + 1)
                if f.square:
                    reached(pe, s.wb_copied, c * E + e - 1)
                else:
                    reached(pe, s.scaled_full, (c * E + e - 1) * f.nb)
                mm(m.wb[e % 2][:, :], g.pick[0:WR, e, :], m.wT[0:WR, par, :], start=True, stop=True).then_inc(s.wb_full, 1)
            if k == 0:
                pe.wait_ge(s.xsplit_ready, c + 1)
            if not (first and k < m.NU):
                pe.wait_ge(s.scaled_full if f.square else s.relu_full, c * NBK + k + 1 - m.NU)
            u = m.up[k % m.NU]
            mm(u[:, :], f.up_hi[:, k, :], m.x_hi[:, par, :], start=True, stop=False)
            mm(u[:, :], f.up_hi[:, k, :], m.x_lo[:, par, :], start=False, stop=False)
            mm(u[:, :], f.up_lo[:, k, :], m.x_hi[:, par, :], start=False, stop=True).then_inc(s.up_full, 1)
            if k >= LAG:
                down(c, par, k - LAG)
            elif not first:
                down(c - 1, 1 - par, k - LAG + NBK)
            if k == AT_XT and not last:
                transpose_x(c + 1)
            if k == AT_Y and not first:
                if not last:
                    pe.wait_ge(s.xT_ready, c + 2)
                transpose_y(c - 1)
            if not last:
                if k == AT_GATE:
                    reached(pe, s.x_done, c)
                    gates(c + 1)
                if k == AT_W:
                    transpose_w(c + 1)

    transpose_x(c0)
    gates(c0)
    transpose_w(c0)
    before_chunks(pe)
    over_pairs(pe, main, c0, NCH)
    for k in range(NBK - LAG, NBK):
        down(c0 + NCH - 1, 1, k)
    transpose_y(c0 + NCH - 1)


def ffn_act(nc, act, s, g, f, m, c0, before_chunks, also=None):
    NBK = E * f.nb

    def copy_xT(c):
        act.wait_ge(s.xT_psum, c + 1)
        reached(act, s.gate_psum, c)
        reached(act, s.xsplit_ready, c)
        nc.scalar.copy(m.xT[:, :], m.misc[:, :]).then_inc(s.xT_ready, 1)

    def gate_exp(c):
        reached(act, s.w_ready, c)
        if f.sigmoid:
            act.wait_ge(s.gate_psum, c + 1)
            nc.scalar.activation(m.gexp[:, :], m.misc[:, 0:CT * E], ACT.Exp, scale=-1.0).then_inc(s.gate_exp, 1)
        else:
            act.wait_ge(s.gate_in, c + 1)
            nc.scalar.activation(m.gexp[:, :], m.gsub[:, :], ACT.Exp).then_inc(s.gate_exp, 1)

    def copy_wT(c, par):
        act.wait_ge(s.wT_psum, c + 1)
        reached(act, s.wb_full, (c - 1) * E)
        if f.b2 is not None:
            reached(act, s.y_full, c - 1)
        nc.scalar.copy(m.wT[0:WR, par, :], m.misc_bf[0:WR, 0:CW]).then_inc(s.wT_ready, 1)

    def copy_y(c):
        if f.b2 is not None:
            act.wait_ge(s.y_full, c + 1)
        act.wait_ge(s.down_done, (c + 1) * NBK)
        reached(act, s.y_psum, c)
        nc.scalar.copy(m.yT[:, :], m.y[:, :]).then_inc(s.yT_ready, 1)

    def hi(c, k, first):
        act.wait_ge(s.scaled_full, c * NBK + k + 1)
        if not (first and k < m.NH):
            act.wait_ge(s.down_done, c * NBK + k + 1 - m.NH)
        q = m.scaled[:, k % m.NS, :]
        nc.scalar.activation(m.h_hi[:, k % m.NH, :], q, ACT.Square if f.square else ACT.Copy).then_inc(s.hi_full, 1)
        if f.square:
            if not (first and k < m.NS):
                lo_ready(act, s, f, c, k - m.NS)
            nc.scalar.activation(m.h[:, k % m.NS, :], q, ACT.Square).then_inc(s.h_full, 1)

    def main(c, par, first, last):
        for k in range(NBK):
            if k == LAG and not first:
                copy_y(c - 1)
            if f.square and k % f.nb == 0:
                e = k // f.nb
                act.wait_ge(s.wb_full, c * E + e + 1)
                if not (first and e < 2):
                    act.wait_ge(s.scaled_full, (c * E + e - 1) * f.nb)
                nc.scalar.copy(m.wb_sb[:, e % 2, :], m.wb[e % 2][:, :]).then_inc(s.wb_copied, 1)
            if not f.square:
                act.wait_ge(s.up_full, c * NBK + k + 1)
                if not (first and k < m.NR):
                    act.wait_ge(s.scaled_full, c * NBK + k + 1 - m.NR)
                nc.scalar.activation(m.relu[:, k % m.NR, :], m.up[k % m.NU][:, :], ACT.Relu,
                                     bias=f.b1[:, k:k + 1]).then_inc(s.relu_full, 1)
            lagged(hi, HI_LAG, NBK, c, k, first)
            if k == AT_SPLIT and also is not None:
                if first:
                    act.wait_ge(also.loaded, 32)
                share = bass.ds(c * CT, CT)
                for raw, hi_part, lo_part in also.weights:
                    i = nc.scalar.copy(hi_part[:, share, :], raw[:, share, :])
                i.then_inc(also.hi_done, 1)
            if not last:
                if k == AT_XT:
                    copy_xT(c + 1)
                if k == AT_EXP:
                    gate_exp(c + 1)
                if k == AT_W:
                    copy_wT(c + 1, 1 - par)

    copy_xT(c0)
    gate_exp(c0)
    copy_wT(c0, 0)
    before_chunks(act)
    over_pairs(act, main, c0, NCH)
    for k in range(NBK - HI_LAG, NBK):
        hi(c0 + NCH - 1, k, False)
    copy_y(c0 + NCH - 1)


def ffn_pool(nc, pool, s, g, f, m, c0):
    NBK = E * f.nb

    def rstd(c):
        pool.wait_ge(s.stats_ready, c + 1)
        reached(pool, s.xn_ready, c)
        nc.gpsimd.tensor_tensor(m.vare[:, :], m.mv[:, :, 1], g.eps[:, 0:CT], ALU.add).then_inc(s.pool_link, 1)
        pool.wait_ge(s.pool_link, c + 1)
        nc.gpsimd.tensor_tensor(m.rstd[:, :], m.vare[:, :], g.neg_half[:, 0:CT], ALU.pow).then_inc(s.rstd_ready, 1)

    def lo(c, k, first):
        pool.wait_ge(s.h_full if f.square else s.hi_full, c * NBK + k + 1)
        if not (first and k < m.NH):
            pool.wait_ge(s.down_done, c * NBK + k + 1 - m.NH)
        h = m.h if f.square else m.scaled
        nc.gpsimd.tensor_tensor(m.h_lo[:, k % m.NH, :], h[:, k % m.NS, :], m.h_hi[:, k % m.NH, :].bitcast(fp32),
                                ALU.subtract).then_inc(s.lo_odd, 1)

    def main(c, par, first, last):
        for k in range(NBK):
            if k == AT_STATS + 1 and not last:
                rstd(c + 1)
            if k % 2:
                lo(c, k, first)

    rstd(c0)
    over_pairs(pool, main, c0, NCH)


def ffn_dve(nc, dve, s, g, f, m, c0, x_before, before_chunks, also=None):
    NBK = E * f.nb
    v = nc.vector

    def stats(c):
        reached(dve, s.rstd_ready, c)
        for t in range(CT):
            i = v.bn_stats(m.bn[:, t, :], g.x[:, bass.ds((c - c0) * CT + t, 1), :][:, 0, :])
        i.then_inc(s.stats_step, 1)

    def aggregate(c):
        for t in range(CT):
            i = v.bn_aggr(m.mv[:, t, :], m.bn[:, t, :])
        i.then_inc(s.stats_ready, 1)

    def norm(c):
        dve.wait_ge(s.rstd_ready, c + 1)
        dve.wait_ge(s.stats_ready, c + 1)
        reached(dve, s.xT_psum, c)
        for t in range(CT):
            i = v.tensor_scalar(m.xn[:, t, :], g.x[:, bass.ds((c - c0) * CT + t, 1), :][:, 0, :], m.mv[:, t, 0:1],
                                m.rstd[:, t:t + 1], ALU.subtract, ALU.mult)
        i.then_inc(s.xn_ready, 1)

    def split(c, par, link):
        dve.wait_ge(s.xT_ready, c + 1)
        reached(dve, s.up_full, (c - 1) * NBK)
        link(v.tensor_copy(m.x_hi[:, par, :], m.xT[:, :]))
        v.tensor_tensor(m.x_lo[:, par, :], m.xT[:, :], m.x_hi[:, par, :].bitcast(fp32), ALU.subtract).then_inc(s.xsplit_ready, 1)

    def route(c, link):
        if f.sigmoid:
            return
        dve.wait_ge(s.gate_psum, c + 1)
        v.tensor_copy(m.glog[:, :, :], m.misc[:, 0:CT * E].rearrange("p (t e) -> p t e", e=E))
        for t in range(CT):
            i = v.max(m.gmax[:, t, :], m.misc[:, t * E:(t + 1) * E])
        link(i)
        reached(dve, s.gate_exp, c)
        v.tensor_tensor(m.gsub[:, :].rearrange("p (t e) -> p t e", e=E), m.glog[:, :, :],
                        m.gmax[:, :, 0:1].broadcast_to([P, CT, E]), ALU.subtract).then_inc(s.gate_in, 1)
        link(v.tensor_tensor(m.chosen[:, :, :], m.glog[:, :, :],
                             m.gmax[:, :, TOP_K - 1:TOP_K].broadcast_to([P, CT, E]), ALU.is_ge))

    def rank_experts(c, link):
        dve.wait_ge(s.gate_exp, c + 1)
        if f.sigmoid:
            link(v.tensor_scalar(m.gsub[:, :], m.gexp[:, :], 1.0, None, ALU.add))
            link(v.reciprocal(m.glog_flat[:, :], m.gsub[:, :]))
            link(v.tensor_tensor(m.biased[:, :, :], m.glog[:, :, :],
                                 f.expert_bias[:, :].unsqueeze(1).broadcast_to([P, CT, E]), ALU.add))
            other = m.biased[:, :, :].unsqueeze(2).broadcast_to([P, CT, E, E])
            own = m.biased[:, :, :].unsqueeze(3).broadcast_to([P, CT, E, E])
            v.tensor_tensor(m.ahead[:, :, :, :], other, own, ALU.is_gt)
            link(v.tensor_tensor(m.tied[:, :, :, :], other, own, ALU.is_equal))
            link(v.tensor_tensor(m.tied[:, :, :, :].rearrange("p t a b -> p t (a b)"),
                                 m.tied[:, :, :, :].rearrange("p t a b -> p t (a b)"),
                                 g.lower[:, :].unsqueeze(1).broadcast_to([P, CT, E * E]), ALU.mult))
            link(v.tensor_tensor(m.ahead[:, :, :, :], m.ahead[:, :, :, :], m.tied[:, :, :, :], ALU.add))
            link(v.tensor_reduce(m.rank[:, :, :], m.ahead[:, :, :, :], AX.X, ALU.add))
        else:
            link(v.tensor_tensor(m.w[:, :, :], m.gexp[:, :].rearrange("p (t e) -> p t e", e=E), m.chosen[:, :, :], ALU.mult))
            link(v.tensor_reduce(m.wsum[:, :], m.w[:, :, :], AX.X, ALU.add))

    def weights(c, link):
        if f.sigmoid:
            link(v.scalar_tensor_tensor(out=m.w[:, :, :], in0=m.rank[:, :, :], scalar=float(TOP_K), in1=m.glog[:, :, :],
                                        op0=ALU.is_lt, op1=ALU.mult))
        else:
            link(v.reciprocal(m.wrec[:, :], m.wsum[:, :]))
            link(v.tensor_tensor(m.w[:, :, :], m.w[:, :, :], m.wrec[:, :].unsqueeze(2).broadcast_to([P, CT, E]), ALU.mult))

    def weight_parts(c, link):
        reached(dve, s.wT_psum, c)
        for a in range(NPARTS):
            i = v.tensor_copy(m.wparts[:, :, :, a, :], m.w[:, :, :].unsqueeze(2).broadcast_to([P, CT, NPARTS, E]))
            if a < NPARTS - 1:
                link(i)
                link(v.tensor_tensor(m.w[:, :, :], m.w[:, :, :], m.wparts[:, :, 0, a, :], ALU.subtract))
        i.then_inc(s.w_ready, 1)

    def update(c):
        dve.wait_ge(s.y_psum, c + 1)
        rows = tiles(g.x, c - c0, CT)
        v.scalar_tensor_tensor(out=rows, in0=m.misc[:, :].rearrange("p (t d) -> p t d", d=D), scalar=f.scale, in1=rows,
                               op0=ALU.mult, op1=ALU.add).then_inc(s.x_done, 1)

    def links_of(c):
        return Link(dve, s.link, c)

    def prepare(c, par, link):
        stats(c)
        dve.wait_ge(s.stats_step, c + 1)
        aggregate(c)
        norm(c)
        split(c, par, link)
        route(c, link)
        rank_experts(c, link)
        weights(c, link)
        weight_parts(c, link)
        link.close()

    def lo(c, k, first):
        if k % 2:
            return
        dve.wait_ge(s.h_full if f.square else s.hi_full, c * NBK + k + 1)
        if not (first and k < m.NH):
            dve.wait_ge(s.down_done, c * NBK + k + 1 - m.NH)
        h = m.h if f.square else m.scaled
        v.tensor_tensor(m.h_lo[:, k % m.NH, :], h[:, k % m.NS, :], m.h_hi[:, k % m.NH, :].bitcast(fp32),
                        ALU.subtract).then_inc(s.lo_even, 1)

    def main(c, par, first, last):
        link = Link(dve, s.link, c + 1)
        for k in range(NBK):
            lagged(lo, LO_LAG, NBK, c, k, first)
            e, hb = divmod(k, f.nb)
            if hb == 0:
                dve.wait_ge(s.wb_copied if f.square else s.wb_full, c * E + e + 1)
            dve.wait_ge(s.up_full if f.square else s.relu_full, c * NBK + k + 1)
            if k == AT_STATS + 1 and not last:
                dve.wait_ge(s.stats_step, c + 2)
            if not (first and k < m.NS):
                dve.wait_ge(s.h_full if f.square else s.hi_full, c * NBK + k + 1 - m.NS)
                if k % 2 and not f.square:
                    lo_ready(dve, s, f, c, k - m.NS)
            scaled = m.scaled[:, k % m.NS, :]
            if f.square:
                i = v.scalar_tensor_tensor(out=scaled, in0=m.up[k % m.NU][:, :], scalar=0.0, in1=m.wb_sb[:, e % 2, :],
                                           op0=ALU.max, op1=ALU.mult)
            else:
                i = v.tensor_tensor(scaled, m.relu[:, k % m.NR, :], m.wb[e % 2][:, :], ALU.mult)
            i.then_inc(s.scaled_full, 1)
            if k == AT_STATS + 1 and not last:
                aggregate(c + 1)
            if k == AT_Y + 1 and not first:
                update(c - 1)
            if k == AT_W and also is not None:
                dve.wait_ge(also.hi_done, c + 1)
                share = bass.ds(c * CT, CT)
                for raw, hi_part, lo_part in also.weights:
                    i = v.tensor_tensor(lo_part[:, share, :], raw[:, share, :], hi_part[:, share, :].bitcast(fp32), ALU.subtract)
                i.then_inc(also.lo_done, 1)
            if not last:
                if k == AT_STATS:
                    stats(c + 1)
                if k == AT_NORM:
                    norm(c + 1)
                if k == AT_SPLIT:
                    split(c + 1, 1 - par, link)
                if k == AT_ROUTE:
                    route(c + 1, link)
                if k == AT_RANK:
                    rank_experts(c + 1, link)
                if k == AT_WEIGHTS:
                    weights(c + 1, link)
                if k == AT_PARTS:
                    weight_parts(c + 1, link)
                    link.close()

    x_before(dve)
    prepare(c0, 0, Link(dve, s.link, c0))
    before_chunks(dve)
    over_pairs(dve, main, c0, NCH)
    for k in range(NBK - LO_LAG, NBK):
        lo(c0 + NCH - 1, k, False)
    update(c0 + NCH - 1)


H = 16
HD = D // H
ST = T // P
SLOT = 32
HPS = P // SLOT
SETS = H // HPS
PAIRS = H // 2
HC = T + P
P2, PV = 4, 5
KQ = 3 * HD
NEG = -1.0e30
LEAST = -3.0e38
ATTN_SEMS = ("stats_step stats_ready pool_link rstd_ready xn_ready xT_psum xT_ready proj_psum proj_copied rotary_step qkv_ready hi_staged lo_staged slots_clear "
             "stage_ready null_prod null_score values_ready kq_psum kq_copied s1_full s1_read slot_step slots_ready max_psum "
             "q2_ready s2_full s2_biased p_raw p_ready pv_done o_copied ob_psum null_in null_exp nulls_ready fin_step "
             "rows_biased att_ready aT_psum aT_ready y_psum x_done o_clear")


def over_sequences(eng, body):
    def has(b, loop=False):
        return group(cur=loop or b < B, nxt=loop or b + 1 < B, prev=loop or 1 <= b <= B, prev2=loop or b >= 2, ever=loop or b > 0)

    body(0, 0, has(0))
    body(1, 1, has(1))
    with eng.Fori(1, B // 2 - 1) as i:
        body(2 * i, 0, has(0, True))
        body(2 * i + 1, 1, has(0, True))
    for b in (B - 2, B - 1, B, B + 1):
        body(b, b % 2, has(b))


def attn_pe(nc, pe, s, g, f, w):
    mm, tr = nc.tensor.matmul, nc.tensor.transpose
    probs_full = s.p_ready if f.null else s.p_raw

    def transpose_x(b, bank):
        pe.wait_ge(s.xn_ready, b + 1)
        for t in range(ST):
            i = tr(bank[:, t * P:(t + 1) * P], w.xn[:, t, :], g.ident[:, :])
        i.then_inc(s.xT_psum, 1)

    def project(b, t, bank):
        pe.wait_ge(s.xT_ready, b + 1)
        mm(bank[:, 0:3 * D], w.xT[:, t * P:(t + 1) * P], f.wqkv[:, :], start=True, stop=True).then_inc(s.proj_psum, 1)

    def transpose_qk(b, par, n, bank):
        jp, qk = n // 2, 1 - n % 2
        pe.wait_ge(s.stage_ready, b + 1)
        pe.wait_ge(s.lo_staged, b + 1)
        src = w.k_stage if qk else w.q_stage[par]
        for jj in range(2):
            for t in range(ST):
                at = jj * T + t * P
                i = tr(bank[:, at:at + P], stage_set(src, t, 2 * jp + jj), g.ident[:, :])
        i.then_inc(s.kq_psum, 1)

    def stage_set(src, t, j):
        return src[:, t, j * HPS:(j + 1) * HPS, :].rearrange("p h r -> p (h r)")

    def transpose_max(b, par, j, bank):
        pe.wait_ge(s.slots_ready, SETS * b + j + 1)
        for t in range(ST):
            i = tr(bank[:, t * P:(t + 1) * P], stage_set(w.q_stage[par], t, j), g.ident[:, :])
        i.then_inc(s.max_psum, 1)

    def pass1(b, par, n, first):
        for hh in range(2):
            j, r = divmod(2 * n + hh, HPS)
            rows = slice(SLOT * r, SLOT * r + KQ)
            if not (first and n == 0):
                pe.wait_ge(s.s1_read, 2 * (PAIRS * b + n - 1) + hh + 1)
            o = w.s1[hh]
            mm(o[:, 0:P], w.qT[rows, par, j, 0:P], w.kT[rows, par, j, 0:P], start=True, stop=True)
            mm(o[:, P:HC], w.qT[rows, par, j, P:T], w.kT[rows, par, j, 0:T], start=True, stop=True).then_inc(s.s1_full, 1)

    def pass2(b, par, n, first):
        done = PAIRS * b + n
        if n % 2 == 0:
            pe.wait_ge(s.q2_ready, SETS * b + n // 2 + 1)
        if not (first and n == 0):
            pe.wait_ge(s.p_raw if f.null else s.s2_biased, done)
        for hh in range(2):
            j, r = divmod(2 * n + hh, HPS)
            rows = slice(SLOT * r, SLOT * r + KQ + 2)
            o = w.s2[hh]
            mm(o[:, 0:T], w.kT[rows, par, j, 0:P], w.q2T[rows, j, 0:T], start=True, stop=True)
            i = mm(o[:, T:HC], w.kT[rows, par, j, P:T], w.q2T[rows, j, P:T], start=True, stop=True)
        i.then_inc(s.s2_full, 1)

    def values(b, par, n):
        if n == 0:
            pe.wait_ge(s.values_ready, b + 1)
        if n in (0, PAIRS // 2):
            reached(pe, s.o_copied, 2 * b + n // (PAIRS // 2))
        pe.wait_ge(probs_full, PAIRS * b + n + 1)
        for hh in range(2):
            h = 2 * n + hh
            j, r = divmod(h, HPS)
            o = w.o[SLOT * r:SLOT * r + w.VC, :]
            at = (j % 2) * T
            pr = w.probs[:, n % w.NPR, hh, :]
            mm(o[:, at:at + T], w.v[:, par, 0, h, :], pr[:, 0:T], start=True, stop=False)
            i = mm(o[:, at + P:at + T], w.v[:, par, 1, h, :], pr[:, T:HC], start=False, stop=True)
        i.then_inc(s.pv_done, 1)

    def transpose_o(b, t, bank):
        pe.wait_ge(s.o_copied, 2 * b + 2)
        for j in range(SETS):
            i = tr(bank[:, j * P:(j + 1) * P], w.oT[:, j, t * P:(t + 1) * P], g.ident[:, :])
        i.then_inc(s.ob_psum, 1)

    def transpose_att(b, bank):
        pe.wait_ge(s.att_ready, b + 1)
        for t in range(ST):
            i = tr(bank[:, t * P:(t + 1) * P], w.att[:, t, :], g.ident[:, :])
        i.then_inc(s.aT_psum, 1)

    def output(b, bank):
        pe.wait_ge(s.aT_ready, b + 1)
        for t in range(ST):
            i = mm(bank[:, t * D:(t + 1) * D], w.aT[:, t * P:(t + 1) * P], f.wo[:, :], start=True, stop=True)
        i.then_inc(s.y_psum, 1)

    m0, m1, m2 = w.misc

    def main(b, par, has):
        q = 1 - par
        for n in range(PAIRS):
            if n < P2 and has.prev:
                pass2(b - 1, q, n + PAIRS - P2, False)
            if n >= P2 and has.cur:
                pass2(b, par, n - P2, not has.ever)
            if has.cur:
                if n == 0:
                    pe.wait_ge(s.kq_copied, 4 * b + 2)
                if n == PAIRS // 2:
                    pe.wait_ge(s.kq_copied, 4 * b + 4)
                pass1(b, par, n, not has.ever)
            if n == 0 and has.prev:
                if has.cur:
                    pe.wait_ge(s.kq_copied, 4 * b + 3)
                transpose_max(b - 1, q, SETS - 1, m0)
            if n == 0 and has.prev2:
                if has.cur:
                    pe.wait_ge(s.kq_copied, 4 * b + 4)
                reached(pe, s.att_ready, b - 1)
                output(b - 2, m1)
            if n == 2 and has.cur:
                pe.wait_ge(s.kq_copied, 4 * b + 2)
                reached(pe, s.aT_ready, b - 1)
                transpose_max(b, par, 0, m2)
            if n == 2 and has.nxt:
                pe.wait_ge(s.kq_copied, 4 * b + 3)
                reached(pe, s.q2_ready, SETS * b)
                transpose_x(b + 1, m0)
            if n == 3 and has.nxt:
                pe.wait_ge(s.kq_copied, 4 * b + 4)
                reached(pe, s.x_done, b - 1)
                project(b + 1, 0, m1)
                pe.wait_ge(s.q2_ready, SETS * b + 1)
                project(b + 1, 1, m2)
            if n == 4 and has.cur:
                if has.nxt:
                    pe.wait_ge(s.xT_ready, b + 2)
                reached(pe, s.q2_ready, SETS * b)
                transpose_max(b, par, 1, m0)
            if n == 5 and has.prev:
                if has.nxt:
                    pe.wait_ge(s.proj_copied, 2 * b + 4)
                if has.cur:
                    pe.wait_ge(s.q2_ready, SETS * b + 1)
                reached(pe, s.x_done, b - 1)
                reached(pe, s.aT_ready, b - 1)
                transpose_o(b - 1, 0, m1)
                transpose_o(b - 1, 1, m2)
            if n == 6 and has.cur:
                pe.wait_ge(s.q2_ready, SETS * b + 2)
                transpose_max(b, par, 2, m0)
            if n == 7 and has.nxt:
                if has.prev:
                    pe.wait_ge(s.att_ready, b)
                pe.wait_ge(s.proj_copied, 2 * b + 4)
                transpose_qk(b + 1, q, 0, m1)
                transpose_qk(b + 1, q, 1, m2)
                pe.wait_ge(s.q2_ready, SETS * b + 3)
                transpose_qk(b + 1, q, 2, m0)
                pe.wait_ge(s.kq_copied, 4 * b + 5)
                transpose_qk(b + 1, q, 3, m1)
            if n == 7 and has.prev:
                if has.nxt:
                    pe.wait_ge(s.kq_copied, 4 * b + 6)
                transpose_att(b - 1, m2)
            if n < PV and has.prev:
                values(b - 1, q, n + PAIRS - PV)
            if n >= PV and has.cur:
                values(b, par, n - PV)

    pe.wait_ge(s.o_clear, 1)
    transpose_x(0, m0)
    project(0, 0, m1)
    project(0, 1, m2)
    pe.wait_ge(s.proj_copied, 2)
    transpose_qk(0, 0, 0, m1)
    transpose_qk(0, 0, 1, m2)
    transpose_qk(0, 0, 2, m0)
    pe.wait_ge(s.kq_copied, 1)
    transpose_qk(0, 0, 3, m1)
    over_sequences(pe, main)


def heads(x):
    return x.rearrange("p t (h d) -> p t h d", d=HD)


def part(x, n):
    return x[:, :, :, n * HD:(n + 1) * HD]


def stage_lo(eng, v, s, w, b, par):
    eng.wait_ge(s.hi_staged, b + 1)
    for n, stage, at in ((0, w.q_stage[par], 1), (1, w.k_stage, 2)):
        i = v.tensor_tensor(part(stage, at).bitcast(fp32r), heads(w.qkv[:, :, n * D:(n + 1) * D]), part(stage, 0), ALU.subtract)
    i.then_inc(s.lo_staged, 1)


def attn_act(nc, act, s, g, f, w):
    m0, m1, m2 = w.misc

    def stage_hi(b, par):
        act.wait_ge(s.qkv_ready, b + 1)
        reached(act, s.max_psum, SETS * (b - 1))
        reached(act, s.kq_psum, 4 * b)
        q, k = heads(w.qkv[:, :, 0:D]), heads(w.qkv[:, :, D:2 * D])
        nc.scalar.copy(part(w.k_stage, 0).bitcast(fp32r), k)
        nc.scalar.copy(part(w.q_stage[par], 0).bitcast(fp32r), q).then_inc(s.hi_staged, 1)
        nc.scalar.copy(part(w.k_stage, 1).bitcast(fp32r), k)
        nc.scalar.copy(part(w.q_stage[par], 2).bitcast(fp32r), q).then_inc(s.stage_ready, 1)

    def place_values(b, par):
        reached(act, s.pv_done, PAIRS * (b - 1))
        nc.scalar.copy(w.v[:, par, :, :, 0:HD], heads(w.qkv[:, :, 2 * D:3 * D])).then_inc(s.values_ready, 1)

    def copy_xT(b):
        act.wait_ge(s.xT_psum, b + 1)
        reached(act, s.proj_psum, 2 * b)
        nc.scalar.copy(w.xT[:, :], m0[:, 0:T]).then_inc(s.xT_ready, 1)

    def copy_projections(b):
        reached(act, s.lo_staged, b)
        if f.null:
            reached(act, s.null_prod, b)
        for t, bank in enumerate((m1, m2)):
            act.wait_ge(s.proj_psum, ST * b + t + 1)
            nc.scalar.copy(w.qkv[:, t, :], bank[:, 0:3 * D]).then_inc(s.proj_copied, 1)

    def copy_kq(b, par):
        for n, bank in enumerate((m1, m2, m0, m1)):
            act.wait_ge(s.kq_psum, 4 * b + n + 1)
            reached(act, *((s.s1_full, H * (b - 1)) if n % 2 else (s.s2_full, PAIRS * (b - 1))))
            to = (w.qT if n % 2 else w.kT)[:, par, n // 2 * 2:n // 2 * 2 + 2, :]
            nc.scalar.copy(to, bank[:, :].rearrange("p (j t) -> p j t", t=T)).then_inc(s.kq_copied, 1)

    def copy_q2(b, j, bank):
        act.wait_ge(s.max_psum, SETS * b + j + 1)
        reached(act, s.s2_full, PAIRS * (b - 1) + 2 * j + 2)
        nc.scalar.copy(w.q2T[:, j, :], bank[:, 0:T]).then_inc(s.q2_ready, 1)

    def exponential(b, n, first):
        if f.null:
            act.wait_ge(s.s2_full, PAIRS * b + n + 1)
        else:
            act.wait_ge(s.s2_biased, PAIRS * b + n + 1)
        if not (first and n < w.NPR):
            act.wait_ge(s.pv_done, PAIRS * b + n + 1 - w.NPR)
        src = w.s2_pair if f.null else w.biased[:, n % w.NB, :, :]
        nc.scalar.activation(w.probs[:, n % w.NPR, :, :], src, ACT.Exp).then_inc(s.p_raw, 1)

    def copy_o(b, half):
        act.wait_ge(s.pv_done, PAIRS * b + (half + 1) * PAIRS // 2)
        reached(act, s.ob_psum, 2 * b)
        nc.scalar.copy(w.oT[:, 2 * half:2 * half + 2, :], w.o[:, :].rearrange("p (j t) -> p j t", t=T)).then_inc(s.o_copied, 1)

    def copy_aT(b):
        act.wait_ge(s.aT_psum, b + 1)
        reached(act, s.y_psum, b)
        nc.scalar.copy(w.aT[:, :], m2[:, 0:T]).then_inc(s.aT_ready, 1)

    def main(b, par, has):
        for n in range(PAIRS):
            if n < P2 and has.prev:
                exponential(b - 1, n + PAIRS - P2, False)
            if n >= P2 and has.cur:
                exponential(b, n - P2, not has.ever)
            if n == 0 and has.prev:
                copy_q2(b - 1, SETS - 1, m0)
                copy_o(b - 1, 0)
                if f.null:
                    act.wait_ge(s.null_in, b)
                    reached(act, s.att_ready, b - 1)
                    nc.scalar.activation(w.null_p[:, :], w.null_d[:, :], ACT.Exp).then_inc(s.null_exp, 1)
            if n == 2 and has.cur:
                copy_q2(b, 0, m2)
            if n == 2 and has.nxt:
                copy_xT(b + 1)
            if n == 3 and has.nxt:
                copy_projections(b + 1)
            if n == 4 and has.prev:
                copy_o(b - 1, 1)
            if n == 4 and has.cur:
                copy_q2(b, 1, m0)
            if n == 6 and has.cur:
                copy_q2(b, 2, m0)
            if n == 5 and has.nxt:
                stage_hi(b + 1, 1 - par)
                place_values(b + 1, 1 - par)
            if n == 7 and has.nxt:
                copy_kq(b + 1, 1 - par)
            if n == 7 and has.prev:
                copy_aT(b - 1)

    act.wait_ge(s.slots_clear, 1)
    copy_xT(0)
    copy_projections(0)
    stage_hi(0, 0)
    place_values(0, 0)
    copy_kq(0, 0)
    over_sequences(act, main)


def attn_pool(nc, pool, s, g, f, w, x_before):
    v = nc.gpsimd

    def rstd(b):
        pool.wait_ge(s.stats_ready, b + 1)
        reached(pool, s.xn_ready, b)
        v.tensor_tensor(w.vare[:, :], w.mv[:, :, 1], g.eps[:, 0:ST], ALU.add).then_inc(s.pool_link, 1)
        pool.wait_ge(s.pool_link, b + 1)
        v.tensor_tensor(w.rstd[:, :], w.vare[:, :], g.neg_half[:, 0:ST], ALU.pow).then_inc(s.rstd_ready, 1)

    def carry():
        v.tensor_tensor(w.carrier[:, :], g.eps[:, 0:1], g.eps[:, 0:1], ALU.mult)

    def complete_projections(b):
        pool.wait_ge(s.proj_copied, 2 * b + 2)
        if f.null:
            geo = w.qkv[:, :, 0:2 * D].rearrange("p t (h d) -> p t h d", d=HD)[:, :, :, HD // 2:]
            quarter = HD // 4
            v.tensor_tensor(w.geo_cos[:, :, :, :], geo, f.cos[:, :, :, :], ALU.mult)
            v.tensor_tensor(w.turned[:, :, :, 0:quarter], geo[:, :, :, quarter:], f.sin[:, :, :, 0:quarter], ALU.mult)
            v.tensor_tensor(w.turned[:, :, :, quarter:], geo[:, :, :, 0:quarter], f.sin[:, :, :, quarter:],
                            ALU.mult).then_inc(s.rotary_step, 1)
            pool.wait_ge(s.rotary_step, b + 1)
            v.tensor_tensor(geo, w.geo_cos[:, :, :, :], w.turned[:, :, :, :], ALU.add).then_inc(s.qkv_ready, 1)
        else:
            v.tensor_tensor(w.qkv[:, :, :], w.qkv[:, :, :], f.bqkv[:, :].unsqueeze(1).broadcast_to([P, ST, 3 * D]),
                            ALU.add).then_inc(s.qkv_ready, 1)

    def null_products(b):
        pool.wait_ge(s.qkv_ready, b + 1)
        reached(pool, s.null_score, b)
        v.tensor_tensor(w.null_qk[:, :, :], w.qkv[:, :, 0:D], f.k_null[:, :].unsqueeze(1).broadcast_to([P, ST, D]),
                        ALU.mult).then_inc(s.null_prod, 1)

    def keep(b, n):
        reached(pool, s.p_ready, PAIRS * b + n)
        pool.wait_ge(s.p_raw, PAIRS * b + n + 1)
        carry()
        pr = w.probs[:, n % w.NPR, :, :]
        for at in (0, T):
            d = pr[:, :, at:at + P]
            i = v.affine_select(out=d, in_=d, pattern=[[0, 2], [1, P]], compare_op=ALU.is_ge, fill=0.0, base=0,
                                channel_multiplier=-1)
        i.then_inc(s.p_ready, 1)

    def null_values(b):
        pool.wait_ge(s.null_exp, b + 1)
        reached(pool, s.att_ready, b)
        v.tensor_tensor(w.nulls[:, :, :, :], f.v_null[:, :].rearrange("p (h d) -> p h d", d=HD).unsqueeze(1).broadcast_to([P, ST, H, HD]),
                        w.null_p[:, :].rearrange("p (t h) -> p t h", h=H).unsqueeze(3).broadcast_to([P, ST, H, HD]),
                        ALU.mult).then_inc(s.nulls_ready, 1)

    def add_output_bias(b):
        pool.wait_ge(s.xn_ready, b + 1)
        rows = tiles(g.x, b, ST)
        v.tensor_tensor(rows, rows, f.bo[:, :].unsqueeze(1).broadcast_to([P, ST, D]), ALU.add).then_inc(s.rows_biased, 1)

    def main(b, par, has):
        for n in range(PAIRS):
            if not f.null and n == 3 and has.nxt:
                add_output_bias(b + 1)
            if f.null:
                if n < P2 and has.prev:
                    keep(b - 1, n + PAIRS - P2)
                if n >= P2 and has.cur:
                    keep(b, n - P2)
                if n == 1 and has.prev:
                    null_values(b - 1)
            if n == 0 and has.nxt:
                rstd(b + 1)
            if n == 3 and has.nxt:
                complete_projections(b + 1)
            if n == 4 and f.null and has.nxt:
                null_products(b + 1)
            if n == 6 and has.nxt and not f.null:
                stage_lo(pool, v, s, w, b + 1, 1 - par)

    x_before(pool)
    v.memset(w.k_stage[:, :, :, KQ:KQ + 2], 1.0)
    v.memset(w.k_stage[:, :, :, KQ + 2:SLOT], 0.0)
    for qs in w.q_stage:
        v.memset(qs[:, :, :, KQ:SLOT], 0.0)
    v.memset(w.v[:, :, :, :, HD:HD + 1], 1.0)
    v.memset(w.v[:, :, :, :, HD + 1:], 0.0).then_inc(s.slots_clear, 1)
    rstd(0)
    complete_projections(0)
    if f.null:
        null_products(0)
    else:
        stage_lo(pool, v, s, w, 0, 0)
        add_output_bias(0)
    over_sequences(pool, main)


def attn_dve(nc, dve, s, g, f, w, x_before):
    v = nc.vector
    m0, m1, m2 = w.misc

    def row(b, t):
        return g.x[:, bass.ds(b * ST + t, 1), :][:, 0, :]

    def stats(b):
        reached(dve, s.rstd_ready, b)
        for t in range(ST):
            i = v.bn_stats(w.bn[:, t, :], row(b, t))
        i.then_inc(s.stats_step, 1)

    def aggregate(b):
        for t in range(ST):
            i = v.bn_aggr(w.mv[:, t, :], w.bn[:, t, :])
        i.then_inc(s.stats_ready, 1)

    def norm(b):
        dve.wait_ge(s.rstd_ready, b + 1)
        dve.wait_ge(s.stats_ready, b + 1)
        reached(dve, s.xT_psum, b)
        for t in range(ST):
            i = v.tensor_scalar(w.xn[:, t, :], row(b, t), w.mv[:, t, 0:1], w.rstd[:, t:t + 1], ALU.subtract, ALU.mult)
        i.then_inc(s.xn_ready, 1)

    def null_scores(b, par):
        dve.wait_ge(s.null_prod, b + 1)
        v.tensor_reduce(w.null_s[:, par, :], w.null_qk[:, :, :].rearrange("p t (h d) -> p (t h) d", d=HD), AX.X,
                        ALU.add).then_inc(s.null_score, 1)

    def maxima(b, par, n):
        if f.null and n == 0:
            dve.wait_ge(s.null_score, b + 1)
        for hh in range(2):
            h = 2 * n + hh
            dve.wait_ge(s.s1_full, H * b + h + 1)
            v.tensor_copy(w.dve_carrier[:, hh:hh + 1], g.eps[:, 0:1])
            for t, (lo, hi) in enumerate(((0, P), (P, HC))):
                least = w.null_s[:, par, t * H + h:t * H + h + 1] if f.null else LEAST
                i = v.tensor_tensor_reduce(out=w.junk[:, hh, lo:hi], in0=w.s1[hh][:, lo:hi], in1=f.bias_q(h, t), scale=1.0,
                                           scalar=least, op0=ALU.add, op1=ALU.max, accum_out=w.top[:, t, h:h + 1])
            i.then_inc(s.s1_read, 1)

    def place_maxima(b, par, j):
        dve.wait_ge(s.s1_read, H * b + (j + 1) * HPS)
        dve.wait_ge(s.kq_psum, 4 * b + 4)
        top = w.top[:, :, j * HPS:(j + 1) * HPS].unsqueeze(3)
        at = w.q_stage[par][:, :, j * HPS:(j + 1) * HPS, :]
        v.tensor_scalar(at[:, :, :, KQ:KQ + 1].bitcast(fp32r), top, -1.0, None, ALU.mult).then_inc(s.slot_step, 1)
        dve.wait_ge(s.slot_step, SETS * b + j + 1)
        v.scalar_tensor_tensor(out=at[:, :, :, KQ + 1:KQ + 2].bitcast(fp32r), in0=top, scalar=-1.0,
                               in1=at[:, :, :, KQ:KQ + 1], op0=ALU.mult, op1=ALU.subtract).then_inc(s.slots_ready, 1)

    def add_bias(b, n, first):
        dve.wait_ge(s.s2_full, PAIRS * b + n + 1)
        if not (first and n < w.NB):
            dve.wait_ge(s.p_raw, PAIRS * b + n + 1 - w.NB)
        v.tensor_tensor(w.biased[:, n % w.NB, :, 0:T], w.s2_pair[:, :, 0:T], f.bias_k(2 * n, T), ALU.add)
        v.tensor_tensor(w.biased[:, n % w.NB, :, T:HC], w.s2_pair[:, :, T:HC], f.bias_k(2 * n, P), ALU.add).then_inc(s.s2_biased, 1)

    def finish(b):
        reached(dve, s.aT_psum, b)
        if f.null:
            dve.wait_ge(s.nulls_ready, b + 1)
        for t, bank in enumerate((m1, m2)):
            dve.wait_ge(s.ob_psum, 2 * b + t + 1)
            sums = bank[:, :].rearrange("p (h d) -> p h d", d=SLOT)
            if f.null:
                v.tensor_tensor(w.den[:, t, :], sums[:, :, HD], w.null_p[:, t * H:(t + 1) * H], ALU.add)
                i = v.tensor_tensor(w.num[:, t, :, :], sums[:, :, 0:HD], w.nulls[:, t, :, :], ALU.add)
            else:
                v.tensor_copy(w.den[:, t, :], sums[:, :, HD])
                i = v.tensor_copy(w.num[:, t, :, :], sums[:, :, 0:HD])
        i.then_inc(s.fin_step, 1)
        dve.wait_ge(s.fin_step, 2 * b + 1)
        v.reciprocal(w.rden[:, :, :], w.den[:, :, :]).then_inc(s.fin_step, 1)
        dve.wait_ge(s.fin_step, 2 * b + 2)
        v.tensor_tensor(w.att[:, :, :].rearrange("p t (h d) -> p (t h) d", d=HD), w.num[:, :, :, :].rearrange("p t h d -> p (t h) d"),
                        w.rden[:, :, :].rearrange("p t h -> p (t h)").unsqueeze(2).broadcast_to([P, ST * H, HD]),
                        ALU.mult).then_inc(s.att_ready, 1)

    def update(b):
        dve.wait_ge(s.y_psum, b + 1)
        if not f.null:
            dve.wait_ge(s.rows_biased, b + 1)
        rows = tiles(g.x, b, ST)
        v.tensor_tensor(rows, m1[:, 0:T].rearrange("p (t d) -> p t d", d=D), rows, ALU.add).then_inc(s.x_done, 1)

    def main(b, par, has):
        for n in range(PAIRS):
            if n == 0 and f.null and has.prev:
                dve.wait_ge(s.s1_read, H * b)
                reached(dve, s.null_exp, b - 1)
                v.tensor_tensor(w.null_d[:, :], w.null_s[:, 1 - par, :], w.top[:, :, :].rearrange("p t h -> p (t h)"),
                                ALU.subtract).then_inc(s.null_in, 1)
                dve.wait_ge(s.null_in, b)
            if not f.null:
                if n < P2 and has.prev:
                    add_bias(b - 1, n + PAIRS - P2, False)
                if n >= P2 and has.cur:
                    add_bias(b, n - P2, not has.ever)
            if n == 0 and has.nxt:
                stats(b + 1)
            if n == 0 and has.nxt:
                dve.wait_ge(s.stats_step, b + 2)
            if has.cur:
                maxima(b, par, n)
                if n % 2:
                    place_maxima(b, par, n // 2)
            if n == 0 and has.nxt:
                aggregate(b + 1)
            if n == 1 and has.nxt:
                norm(b + 1)
            if n == 1 and has.prev2:
                update(b - 2)
            if n == 6 and has.nxt and f.null:
                stage_lo(dve, v, s, w, b + 1, 1 - par)
            if n == 5 and f.null and has.nxt:
                null_scores(b + 1, 1 - par)
            if n == 5 and has.prev:
                finish(b - 1)

    x_before(dve)
    v.memset(w.o[:, :], 0.0).then_inc(s.o_clear, 1)
    stats(0)
    dve.wait_ge(s.stats_step, 1)
    aggregate(0)
    norm(0)
    if f.null:
        stage_lo(dve, v, s, w, 0, 0)
        null_scores(0, 0)
    over_sequences(dve, main)


def program(nc, a, out, stages=("ffn0", "attn0", "ffn0", "ffn1", "attn1", "ffn1")):
    ctx = ExitStack()
    with ctx:
        def sb(name, shape, dt=fp32, stack=ctx):
            return stack.enter_context(nc.sbuf_tensor(name, shape, dt))

        def sem(name):
            return ctx.enter_context(nc.semaphore(name))

        pair = ctx.enter_context(nc.psum_tensor("bank_pair", [P, 2, 512], fp32))
        banks = [ctx.enter_context(nc.psum_tensor(f"bank{i}", [P, 512], fp32)) for i in range(6)]
        banks[2:2] = [pair[:, 0, :], pair[:, 1, :]]

        g = group(
            x=sb("x", [P, B * T // P, D]), ident=sb("ident", [P, P]), ident_bf=sb("ident_bf", [P, P], bf16),
            pick=sb("pick", [WR, E, P], bf16), lower=sb("lower", [P, E * E]),
            neg_half=sb("neg_half", [P, CT]), eps=sb("eps", [P, CT]))

        def split_matrices(name, n, stack):
            hi = sb(f"{name}_hi", [P, n, P], fp32r, stack)
            with ExitStack() as short:
                raw = sb(f"{name}_raw", [P, n, P], fp32, short)
            return raw, hi, sb(f"{name}_lo", [P, n, P], fp32r, stack)

        def ffn_weights(name, nb, stack=ctx):
            gate = sb(f"{name}_gate", [P, E])
            up, down = (split_matrices(f"{name}_{x}", E * nb, stack) for x in ("up", "down"))
            return dict(nb=nb, gate=gate, up=up, up_hi=up[1], up_lo=up[2], down=down, down_hi=down[1], down_lo=down[2])

        f1 = group(**ffn_weights("ffn1", 4), sigmoid=False, square=False, b1=sb("b1", [P, 4 * E]),
                             b2=sb("b2_split", [WR, D], bf16), scale=0.5 / E)
        mask = sb("mask", [P, T])
        a0 = group(null=True, wqkv=sb("wqkv0", [P, 3 * D]), wo=sb("wo0", [P, D]), k_null=sb("k_null", [P, D]),
                   v_null=sb("v_null", [P, D]), cos=sb("cos", [P, ST, 2 * H, HD // 2]), sin=sb("sin", [P, ST, 2 * H, HD // 2]),
                   bias_q=lambda h, t: mask[:, :] if t else mask[:, P:T])
        expert_bias = sb("expert_bias", [P, E])
        with ExitStack() as own:
            f0 = group(**ffn_weights("ffn0", 2, own), sigmoid=True, square=True, b1=None, b2=None, scale=0.5,
                                 expert_bias=expert_bias)
        table_k = sb("table_k", [P, H, T])
        table_q = sb("table_q", [P, H, T])
        a1 = group(null=False, wqkv=sb("wqkv1", [P, 3 * D]), wo=sb("wo1", [P, D]), bqkv=sb("bqkv", [P, 3 * D]),
                   bo=sb("bo", [P, D]), bias_q=lambda h, t: table_q[:, h, :] if t else table_q[:, h, P:T],
                   bias_k=lambda h, n: table_k[:, h:h + 2, 0:n])

        stack = ExitStack()

        def fb(name, shape, dt=fp32):
            return sb(name, shape, dt, stack)

        m = Buffers()
        m.NU, m.NR, m.NS, m.NH = 4, 4, 4, 4
        m.up, m.wb, m.y, m.misc = banks[0:4], banks[4:6], banks[6], banks[7]
        m.misc_bf = m.misc[:, :].bitcast(bf16)
        m.bn, m.mv = fb("bn", [P, CT, 6]), fb("mv", [P, CT, 2])
        m.vare, m.rstd = fb("vare", [P, CT]), fb("rstd", [P, CT])
        m.xn, m.xT = fb("xn", [P, CT, D]), fb("xT", [P, CW])
        m.x_hi, m.x_lo = fb("x_hi", [P, 2, CW], fp32r), fb("x_lo", [P, 2, CW], fp32r)
        m.gexp, m.gsub, m.glog = fb("gexp", [P, CT * E]), fb("gsub", [P, CT * E]), fb("glog", [P, CT, E])
        m.glog_flat = m.glog[:, :, :].rearrange("p t e -> p (t e)")
        m.gmax, m.chosen, m.biased = fb("gmax", [P, CT, 8]), fb("chosen", [P, CT, E]), fb("biased", [P, CT, E])
        m.ahead, m.tied = fb("ahead", [P, CT, E, E]), fb("tied", [P, CT, E, E])
        m.rank, m.w = fb("rank", [P, CT, E]), fb("w", [P, CT, E])
        m.wsum, m.wrec = fb("wsum", [P, CT]), fb("wrec", [P, CT])
        m.wparts = fb("wparts", [P, CT, NPARTS, NPARTS, E], bf16)
        m.wparts_flat = m.wparts[:, :, :, :, :].rearrange("p t b a e -> p t (b a e)")
        m.wT = fb("wT", [WR, 2, CW], bf16)
        m.relu, m.scaled, m.h = fb("relu", [P, m.NR, CW]), fb("scaled", [P, m.NS, CW]), fb("h", [P, m.NS, CW])
        m.wb_sb = m.relu
        m.h_hi, m.h_lo = fb("h_hi", [P, m.NH, CW], fp32r), fb("h_lo", [P, m.NH, CW], fp32r)
        m.yT = fb("yT", [P, CW])
        pick_f, part_rows = fb("pick_f", [WR, E, P]), fb("part_rows", [WR, NPARTS])
        b2_rows, b2_part, b2_sum = fb("b2_rows", [WR, D]), fb("b2_part", [WR, D], bf16), fb("b2_sum", [WR, D])
        rel, flip, distance = fb("rel", [P, D]), fb("flip", [P, P]), fb("distance", [P, H])
        curves = fb("curves", [H, 4, T])
        curves_dram = nc.dram_tensor("curves_dram", (H, 4, P, T), fp32, kind="Internal")
        stack.close()

        stack = ExitStack()
        w = Buffers()
        w.VC, w.NPR, w.NB = 2 * HD, 2, 1
        w.s1, w.s2, w.o, w.misc, w.s2_pair = banks[0:2], banks[2:4], banks[4], banks[5:8], pair[:, :, 0:HC]
        w.bn, w.mv = fb("abn", [P, ST, 6]), fb("amv", [P, ST, 2])
        w.vare, w.rstd = fb("avare", [P, ST]), fb("arstd", [P, ST])
        w.xn, w.xT, w.qkv = fb("axn", [P, ST, D]), fb("axT", [P, T]), fb("qkv", [P, ST, 3 * D])
        w.turned, w.geo_cos = fb("turned", [P, ST, 2 * H, HD // 2]), fb("geo_cos", [P, ST, 2 * H, HD // 2])
        w.q_stage = [fb(f"q_stage{i}", [P, ST, H, SLOT]) for i in range(2)]
        w.k_stage = fb("k_stage", [P, ST, H, SLOT])
        w.qT, w.kT = fb("qT", [P, 2, SETS, T], fp32r), fb("kT", [P, 2, SETS, T], fp32r)
        w.q2T = fb("q2T", [P, SETS, T], fp32r)
        w.v = fb("v", [P, 2, ST, H, w.VC])
        w.junk, w.top = fb("junk", [P, 2, HC]), fb("top", [P, ST, H])
        w.null_qk, w.null_s = fb("null_qk", [P, ST, D]), fb("null_s", [P, 2, ST * H])
        w.null_d, w.null_p = fb("null_d", [P, ST * H]), fb("null_p", [P, ST * H])
        w.nulls, w.num = fb("nulls", [P, ST, H, HD]), fb("num", [P, ST, H, HD])
        w.den, w.rden = fb("den", [P, ST, H]), fb("rden", [P, ST, H])
        w.biased = fb("biased_scores", [P, w.NB, 2, HC])
        w.probs = fb("probs", [P, w.NPR, 2, HC])
        w.carrier, w.dve_carrier = fb("carrier", [P, 1]), fb("dve_carrier", [P, 2])
        w.oT, w.att, w.aT = fb("oT", [P, SETS, T]), fb("att", [P, ST, D]), fb("aT", [P, T])
        stack.close()

        load_first_rows, load_x, load_const, load_later, load_up0, load_down0, load_ffn1, load_attn, load_tables = (
            sem(n) for n in "load_first_rows load_x load_const load_later load_up0 load_down0 load_ffn1 load_attn load_tables".split())
        const_ready, b2_step, ffn0_hi, ffn0_lo, ffn1_hi, ffn1_lo = (
            sem(n) for n in "const_ready b2_step ffn0_hi ffn0_lo ffn1_hi ffn1_lo".split())
        distance_sum, curve_psum, curves_ready, curves_stored, scaled_qkv, stored = (
            sem(n) for n in "distance_sum curve_psum curves_ready curves_stored scaled_qkv stored".split())

        layer_kinds = ("ffn0", "ffn1")
        unused = {"ffn0": "gate_in relu_full", "ffn1": "h_full wb_copied", "attn0": "rows_biased s2_biased",
                  "attn1": "null_prod null_score null_in null_exp nulls_ready p_ready rotary_step"}
        sems = {kind: group(**{x: sem(f"{kind}_{x}") for x in (FFN_SEMS if kind in ("ffn0", "ffn1") else ATTN_SEMS).split()
                                         if x not in unused[kind].split()}) for kind in dict.fromkeys(stages)}
        plan = [(kind, sems[kind], stages[:n].count(kind) * (NCH if kind in layer_kinds else B)) for n, kind in enumerate(stages)]
        layer = {"ffn0": f0, "ffn1": f1}
        attn = {"attn0": a0, "attn1": a1}
        split_ffn1 = group(weights=(f1.up, f1.down), hi_done=ffn1_hi, lo_done=ffn1_lo, loaded=load_ffn1)

        def after_stage(n):
            if n <= 0:
                return lambda eng: eng.wait_ge(load_first_rows, 16)
            kind, s, c0 = plan[n - 1]
            return lambda eng: eng.wait_ge(s.x_done, c0 + (NCH if kind in layer_kinds else B))

        x_rows = a["x"].rearrange("(t p) d -> p t d", p=P)
        out_rows = out.rearrange("(t p) d -> p t d", p=P)

        def matrices(name, cols):
            return a[name].rearrange("p (n m) -> p n m", m=cols)

        constants = ((g.ident, "ident"), (g.neg_half, "neg_half"), (g.eps, "eps"), (f0.gate, "gate0"), (g.lower, "lower"),
                     (f0.expert_bias, "expert_bias"), (pick_f, "pick"))
        later_constants = ((part_rows, "part_rows"), (b2_rows, "b2"), (f1.b1, "b1"), (f1.gate, "gate1"), (flip, "flip"), (rel, "rel"))
        for_attention = ((a0.wqkv, "wqkv0"), (a0.wo, "wo0"), (a0.k_null, "k_null"), (a0.v_null, "v_null"), (a0.cos, "cos"),
                         (a0.sin, "sin"), (mask, "mask"), (a1.wqkv, "wqkv1"), (a1.wo, "wo1"),
                         (a1.bqkv, "bqkv"), (a1.bo, "bo"))

        def nothing(eng):
            pass

        block = ctx.enter_context(nc.Block())

        @block.sync
        def _(sp):
            sp.dma_start(tiles(g.x, 0, CT), x_rows[:, 0:CT, :]).then_inc(load_first_rows, 16)
            for dst, name in constants:
                sp.dma_start(whole(dst), a[name]).then_inc(load_const, 16)
            for dst, name in later_constants:
                sp.dma_start(whole(dst), a[name]).then_inc(load_later, 16)
            for (raw, _, _), name, loaded in ((f0.up, "up0", load_up0), (f0.down, "down0", load_down0)):
                sp.dma_start(raw[:, :, :], matrices(name, P)).then_inc(loaded, 16)
            sp.dma_start(g.x[:, CT:, :], x_rows[:, CT:, :]).then_inc(load_x, 16)
            for (raw, _, _), name in ((f1.up, "up1"), (f1.down, "down1")):
                sp.dma_start(raw[:, :, :], matrices(name, P)).then_inc(load_ffn1, 16)
            for dst, name in for_attention:
                sp.dma_start(whole(dst), a[name]).then_inc(load_attn, 16)
            sp.wait_ge(curves_ready, 1)
            for n in range(4):
                sp.dma_start(curves_dram[:, n, :, :], curves[:, n:n + 1, :].broadcast_to([H, P, T])).then_inc(curves_stored, 16)
            sp.wait_ge(curves_stored, 64)
            if "attn1" in stages:
                uses = [n + 1 for n, kind in enumerate(stages) if kind == "ffn0"]
                if uses:
                    after_stage(uses[-1])(sp)
                for table, first in ((table_k, 0), (table_q, 2)):
                    for kind in range(2):
                        shifted = bass.AP(curves_dram, (first + kind) * P * T + P - 1, [[T - 1, P], [4 * P * T, H], [1, P]])
                        sp.dma_start(table[:, :, kind * P:(kind + 1) * P], shifted).then_inc(load_tables, 16)
            kind, s, c0 = plan[-1]
            per = CT if kind in layer_kinds else ST
            for c in range(B * T // P // per):
                sp.wait_ge(s.x_done, c0 + c + 1)
                sp.dma_start(out_rows[:, c * per:(c + 1) * per, :], tiles(g.x, c, per)).then_inc(stored, 16)
            sp.wait_ge(stored, 16 * (B * T // P // per))

        @block.vector
        def _(dve):
            v = nc.vector
            dve.wait_ge(load_const, 16 * len(constants))
            v.tensor_copy(g.ident_bf[:, :], g.ident[:, :])
            v.tensor_copy(g.pick[:, :, :], pick_f[:, :, :]).then_inc(const_ready, 1)

            def prepare_later_stages():
                dve.wait_ge(load_later, 16 * len(later_constants))
                v.tensor_scalar(b2_sum[:, :], b2_rows[:, :], 0.0, None, ALU.mult)
                for n in range(NPARTS):
                    v.tensor_copy(b2_part[:, :], b2_rows[:, :]).then_inc(b2_step, 1)
                    dve.wait_ge(b2_step, 2 * n + 1)
                    v.scalar_tensor_tensor(out=b2_sum[:, :], in0=b2_part[:, :], scalar=part_rows[:, n:n + 1], in1=b2_sum[:, :],
                                           op0=ALU.mult, op1=ALU.add)
                    v.tensor_tensor(b2_rows[:, :], b2_rows[:, :], b2_part[:, :], ALU.subtract).then_inc(b2_step, 1)
                    dve.wait_ge(b2_step, 2 * n + 2)
                v.tensor_copy(f1.b2[:, :], b2_sum[:, :]).then_inc(const_ready, 1)
                v.tensor_reduce(distance[:, :], rel[:, :].rearrange("p (h d) -> p h d", d=HD), AX.X, ALU.add).then_inc(distance_sum, 1)
                dve.wait_ge(curve_psum, 1)
                near, far = banks[5][0:H, 0:P], banks[5][0:H, P:2 * P]
                last = near[:, P - 1:P]
                v.memset(curves[:, 0, 0:P - 1], NEG)
                v.tensor_copy(curves[:, 0, P - 1:2 * P - 1], near)
                v.memset(curves[:, 0, 2 * P - 1:], 0.0)
                v.tensor_copy(curves[:, 1, 0:P - 1], near[:, 1:P])
                v.tensor_copy(curves[:, 1, P - 1:], last.broadcast_to([H, P + 1]))
                v.tensor_copy(curves[:, 2, 0:P + 1], last.broadcast_to([H, P + 1]))
                v.tensor_copy(curves[:, 2, P + 1:], far[:, 1:P])
                v.tensor_copy(curves[:, 3, 0:P], far)
                v.memset(curves[:, 3, P:], NEG).then_inc(curves_ready, 1)

            def before_chunks(dve):
                dve.wait_ge(load_x, 16)
                prepare_later_stages()
                for n, (raw, hi, lo) in enumerate((f0.up, f0.down)):
                    dve.wait_ge(ffn0_hi, n + 1)
                    v.tensor_tensor(lo[:, :, :], raw[:, :, :], hi[:, :, :].bitcast(fp32), ALU.subtract).then_inc(ffn0_lo, 1)

            def scale_queries():
                dve.wait_ge(load_attn, 16 * len(for_attention))
                v.tensor_scalar(a0.wqkv[:, 0:D], a0.wqkv[:, 0:D], float(HD // 2) ** -0.5, None, ALU.mult)
                v.tensor_scalar(a1.wqkv[:, 0:D], a1.wqkv[:, 0:D], float(HD) ** -0.5, None, ALU.mult)
                v.tensor_scalar(a1.bqkv[:, 0:D], a1.bqkv[:, 0:D], float(HD) ** -0.5, None, ALU.mult).then_inc(scaled_qkv, 1)

            for n, (kind, s, c0) in enumerate(plan):
                if kind in layer_kinds:
                    ffn_dve(nc, dve, s, g, layer[kind], m, c0, after_stage(n), nothing if n else before_chunks, None if n else split_ffn1)
                else:
                    if kind == "attn1":
                        dve.wait_ge(load_tables, 64)
                    else:
                        scale_queries()
                        dve.wait_ge(curves_stored, 64)
                    attn_dve(nc, dve, s, g, attn[kind], w, after_stage(n))

        @block.scalar
        def _(act):
            def before_chunks(act):
                for n, (raw, hi, lo) in enumerate((f0.up, f0.down)):
                    act.wait_ge((load_up0, load_down0)[n], 16)
                    nc.scalar.copy(hi[:, :, :], raw[:, :, :]).then_inc(ffn0_hi, 1)

            act.wait_ge(load_const, 16 * len(constants))
            for n, (kind, s, c0) in enumerate(plan):
                if kind in layer_kinds:
                    ffn_act(nc, act, s, g, layer[kind], m, c0, nothing if n else before_chunks, None if n else split_ffn1)
                else:
                    attn_act(nc, act, s, g, attn[kind], w)

        @block.gpsimd
        def _(pool):
            pool.wait_ge(load_const, 16 * len(constants))
            for n, (kind, s, c0) in enumerate(plan):
                if kind in layer_kinds:
                    ffn_pool(nc, pool, s, g, layer[kind], m, c0)
                else:
                    pool.wait_ge(load_attn, 16 * len(for_attention))
                    pool.wait_ge(curves_stored, 64)
                    attn_pool(nc, pool, s, g, attn[kind], w, after_stage(n))

        @block.tensor
        def _(pe):
            pe.wait_ge(load_const, 16 * len(constants))
            pe.wait_ge(const_ready, 1)

            def before_chunks(pe):
                pe.wait_ge(const_ready, 2)
                pe.wait_ge(distance_sum, 1)
                nc.tensor.matmul(banks[5][0:H, 0:P], distance[:, :], g.ident[:, :], start=True, stop=True)
                nc.tensor.matmul(banks[5][0:H, P:2 * P], distance[:, :], flip[:, :], start=True, stop=True).then_inc(curve_psum, 1)
                pe.wait_ge(curves_ready, 1)
                pe.wait_ge(ffn0_lo, 2)

            for n, (kind, s, c0) in enumerate(plan):
                if kind == "ffn1":
                    pe.wait_ge(ffn1_lo, NCH)
                if n > 0:
                    after_stage(n)(pe)
                if kind in layer_kinds:
                    ffn_pe(nc, pe, s, g, layer[kind], m, c0, nothing if n else before_chunks)
                else:
                    pe.wait_ge(scaled_qkv, 1)
                    attn_pe(nc, pe, s, g, attn[kind], w)


def whole(t):
    return {2: lambda: t[:, :], 3: lambda: t[:, :, :], 4: lambda: t[:, :, :, :]}[len(t.shape)]()


def layouts(i):
    def c(v):
        return np.ascontiguousarray(v)

    def rows(v):
        return c(np.broadcast_to(v.reshape(1, -1), (P, v.size)))

    def by_head(sem, geo):
        n = sem.shape[0]
        return np.concatenate([sem.reshape(n, H, -1), geo.reshape(n, H, -1)], axis=2).reshape(n, D)

    eye = np.eye(P, dtype=np.float32)
    pick = np.zeros((WR, E, P), np.float32)
    for n in range(NPARTS):
        for e in range(E):
            pick[n * E + e, e] = 1.0
    part_rows = np.zeros((WR, NPARTS), np.float32)
    for n in range(NPARTS):
        part_rows[n * NPARTS * E:(n + 1) * NPARTS * E, n] = 1.0
    h0, h1 = i["L0_ffn_w_up"].shape[1], i["L1_ffn_W1"].shape[2]

    geo_hd = i["L0_attn_wq_geo"].shape[1] // H
    inv_freq = (1.0 / np.float32(10000.0) ** (np.arange(0, geo_hd, 2, dtype=np.float32) / np.float32(geo_hd))).astype(np.float32)
    angle = (np.arange(T, dtype=np.float32)[:, None] * inv_freq[None, :]).astype(np.float32)
    cs, sn = np.cos(angle), np.sin(angle)
    cos = np.zeros((T, 2, H, HD // 2), np.float32)
    cos[..., 0:2] = cos[..., 2:4] = cs[:, None, None, :]
    sin = np.zeros((T, 2, H, HD // 2), np.float32)
    sin[..., 0:2], sin[..., 2:4] = -sn[:, None, None, :], sn[:, None, None, :]
    tiled = lambda v: c(v.reshape(ST, P, -1).transpose(1, 0, 2))
    lower = np.tril(np.ones((P, P), np.float32))
    return dict(
        x=i["L0_attn_x"].reshape(B * T, D), ident=eye, flip=c(eye[::-1]), pick=pick, part_rows=part_rows,
        lower=rows(np.tril(np.ones((E, E), np.float32), -1)),
        eps=np.full((P, CT), LN_EPS, np.float32), neg_half=np.full((P, CT), -0.5, np.float32),
        gate0=c(i["L0_ffn_gate_w"].T), expert_bias=rows(i["L0_ffn_expert_bias"]),
        up0=c(i["L0_ffn_w_up"].transpose(2, 0, 1)).reshape(D, E * h0),
        down0=c(i["L0_ffn_w_down"].transpose(0, 2, 1).reshape(E * h0 // P, P, D).transpose(1, 0, 2)).reshape(P, -1),
        gate1=i["L1_ffn_W_gate"], up1=c(i["L1_ffn_W1"].transpose(1, 0, 2)).reshape(D, E * h1),
        down1=c(i["L1_ffn_W2"].reshape(E * h1 // P, P, D).transpose(1, 0, 2)).reshape(P, -1),
        b1=c(i["L1_ffn_b1"].reshape(E * h1 // P, P).T), b2=c(np.tile(i["L1_ffn_b2"], (NPARTS * NPARTS, 1))),
        wqkv0=c(np.concatenate([by_head(i["L0_attn_wq_sem"], i["L0_attn_wq_geo"]),
                                by_head(i["L0_attn_wk_sem"], i["L0_attn_wk_geo"]), i["L0_attn_wv"]], axis=1)),
        wo0=i["L0_attn_wo"], k_null=rows(by_head(i["L0_attn_k_sem_null"][None], i["L0_attn_k_geo_null"][None])),
        v_null=rows(i["L0_attn_v_null"]), cos=tiled(cos).reshape(P, ST, 2 * H, HD // 2), sin=tiled(sin).reshape(P, ST, 2 * H, HD // 2),
        mask=c(np.concatenate([np.zeros((P, P), np.float32), np.where(lower > 0, np.float32(0), np.float32(NEG))], axis=1)),
        wqkv1=c(i["L1_attn_qkv_w"].T), wo1=c(i["L1_attn_proj_w"].T), bqkv=rows(i["L1_attn_qkv_b"]), bo=rows(i["L1_attn_proj_b"]),
        rel=c(i["L1_attn_rel_pos_emb"][P - 1:]),
    )


def kernel(**inputs):
    import concourse.bacc as bacc
    from concourse.bass_utils import run_bass_kernel_spmd

    arrays = layouts({n: np.asarray(v) for n, v in inputs.items()})
    nc = bacc.Bacc("TRN2", target_bir_lowering=False, num_devices=1)
    a = {n: nc.dram_tensor(f"in_{n}", v.shape, fp32, kind="ExternalInput").ap() for n, v in arrays.items()}
    out = nc.dram_tensor("out", (B * T, D), fp32, kind="ExternalOutput").ap()
    program(nc, a, out)
    r = run_bass_kernel_spmd(nc, [{f"in_{n}": v for n, v in arrays.items()}], core_ids=[0])
    return r.results[0]["out"].reshape(B, T, D)
```
